# Optimizing a Trainium2 kernel written in Bass

```python
import numpy as np
import jax
import jax.numpy as jnp

def _softmax(x, axis=-1):
    return jax.nn.softmax(x, axis=axis)

def _gelu(x):
    return jax.nn.gelu(x, approximate=True)

def _silu(x):
    return jax.nn.silu(x)

def _sigmoid(x):
    return jax.nn.sigmoid(x)

def _layernorm(x, axis=-1, eps=1e-05):
    m = jnp.mean(x, axis=axis, keepdims=True)
    v = jnp.var(x, axis=axis, keepdims=True)
    return (x - m) / jnp.sqrt(v + eps)

def _scatter_add(tgt, idx, src, axis=0):
    return tgt.at[idx].add(src)

def _segment_sum(src, seg, n):
    return jax.ops.segment_sum(src, seg, n)
kernel_name = 'mk_seq_postln_d1_jaxref_r8_b71119'

def setup_inputs(seed: int=0):
    np.random.seed(seed)
    _w = jnp.asarray

    def _L0_attn_setup():
        import jax, jax.numpy as jnp
        import numpy as np
        HID = 128
        NH = 16
        HD = HID // NH
        RANK = 16
        B, L = (2, 256)
        key = jax.random.key(seed)
        ks = jax.random.split(key, 9)
        s = 0.02
        return {'x': jax.random.normal(ks[0], (B, L, HID), dtype=jnp.float32), 'Wq': jax.random.normal(ks[1], (HID, HID), dtype=jnp.float32) * s, 'Wk': jax.random.normal(ks[2], (HID, HID), dtype=jnp.float32) * s, 'Wv': jax.random.normal(ks[3], (HID, HID), dtype=jnp.float32) * s, 'Wg': jax.random.normal(ks[4], (HID, HID), dtype=jnp.float32) * s, 'Wgk1': jax.random.normal(ks[5], (HID, RANK), dtype=jnp.float32) * s, 'Wgk2': jax.random.normal(ks[6], (RANK, HID), dtype=jnp.float32) * s, 'bgk2': jnp.zeros((HID,), dtype=jnp.float32), 'gamma': jnp.ones((HID,), dtype=jnp.float32), 'beta': jnp.zeros((HID,), dtype=jnp.float32), 'Wout': jax.random.normal(ks[7], (HID, HID), dtype=jnp.float32) * s}
    _L0_attn_in = _L0_attn_setup()

    def _L0_ffn_setup():
        import jax, jax.numpy as jnp
        import numpy as np
        D_IN, D_HID = (128, 512)

        def _ternary(key, shape):
            return jax.random.randint(key, shape, -1, 2).astype(jnp.float32)

        def _tlin(x, w, s):
            return jnp.einsum('bsi,oi->bso', x, w) * s
        key = jax.random.key(seed)
        ks = jax.random.split(key, 12)
        inv = lambda fan: 1.0 / np.sqrt(fan).astype(np.float32)
        return {'x': jax.random.normal(ks[0], (4, 256, D_IN), dtype=jnp.float32), 'w1_w': _ternary(ks[1], (D_HID, D_IN)), 'w1_s': jax.random.uniform(ks[2], (D_HID,), dtype=jnp.float32) * inv(D_IN), 'w2_w': _ternary(ks[3], (D_HID, D_IN)), 'w2_s': jax.random.uniform(ks[4], (D_HID,), dtype=jnp.float32) * inv(D_IN), 'h1_w': _ternary(ks[5], (D_HID, D_HID)), 'h1_s': jax.random.uniform(ks[6], (D_HID,), dtype=jnp.float32) * inv(D_HID), 'h2_w': _ternary(ks[7], (D_HID, D_HID)), 'h2_s': jax.random.uniform(ks[8], (D_HID,), dtype=jnp.float32) * inv(D_HID), 'w3_w': _ternary(ks[9], (D_IN, D_HID)), 'w3_s': jax.random.uniform(ks[10], (D_IN,), dtype=jnp.float32) * inv(D_HID)}
    _L0_ffn_in = _L0_ffn_setup()
    _d = {'L0_attn_x': _L0_attn_in['x'], 'L0_attn_Wq': _L0_attn_in['Wq'], 'L0_attn_Wk': _L0_attn_in['Wk'], 'L0_attn_Wv': _L0_attn_in['Wv'], 'L0_attn_Wg': _L0_attn_in['Wg'], 'L0_attn_Wgk1': _L0_attn_in['Wgk1'], 'L0_attn_Wgk2': _L0_attn_in['Wgk2'], 'L0_attn_bgk2': _L0_attn_in['bgk2'], 'L0_attn_gamma': _L0_attn_in['gamma'], 'L0_attn_beta': _L0_attn_in['beta'], 'L0_attn_Wout': _L0_attn_in['Wout'], 'L0_ffn_w1_w': _L0_ffn_in['w1_w'], 'L0_ffn_w1_s': _L0_ffn_in['w1_s'], 'L0_ffn_w2_w': _L0_ffn_in['w2_w'], 'L0_ffn_w2_s': _L0_ffn_in['w2_s'], 'L0_ffn_h1_w': _L0_ffn_in['h1_w'], 'L0_ffn_h1_s': _L0_ffn_in['h1_s'], 'L0_ffn_h2_w': _L0_ffn_in['h2_w'], 'L0_ffn_h2_s': _L0_ffn_in['h2_s'], 'L0_ffn_w3_w': _L0_ffn_in['w3_w'], 'L0_ffn_w3_s': _L0_ffn_in['w3_s']}
    _x0 = _d['L0_attn_x']
    _d['L0_attn_x'] = jax.random.normal(jax.random.fold_in(jax.random.key(seed), 1), (4, 512, 128), dtype=_x0.dtype)
    del _x0
    return _d

def reference(L0_attn_x, L0_attn_Wq, L0_attn_Wk, L0_attn_Wv, L0_attn_Wg, L0_attn_Wgk1, L0_attn_Wgk2, L0_attn_bgk2, L0_attn_gamma, L0_attn_beta, L0_attn_Wout, L0_ffn_w1_w, L0_ffn_w1_s, L0_ffn_w2_w, L0_ffn_w2_s, L0_ffn_h1_w, L0_ffn_h1_s, L0_ffn_h2_w, L0_ffn_h2_s, L0_ffn_w3_w, L0_ffn_w3_s):

    def _L0_attn_ref(x, Wq, Wk, Wv, Wg, Wgk1, Wgk2, bgk2, gamma, beta, Wout):
        import jax, jax.numpy as jnp
        import numpy as np
        HID = 128
        NH = 16
        HD = HID // NH
        RANK = 16
        B, L = (2, 256)
        Bb, Ll, Hid = x.shape
        H, Dh = (NH, HD)
        q = (x @ Wq).reshape(Bb, Ll, H, Dh)
        k = (x @ Wk).reshape(Bb, Ll, H, Dh)
        v = (x @ Wv).reshape(Bb, Ll, H, Dh)
        gk = (jax.nn.log_sigmoid(x @ Wgk1 @ Wgk2 + bgk2) / 16.0).reshape(Bb, Ll, H, Dh)
        qT = jnp.transpose(q, (1, 0, 2, 3))
        kT = jnp.transpose(k, (1, 0, 2, 3))
        vT = jnp.transpose(v, (1, 0, 2, 3))
        gT = jnp.transpose(gk, (1, 0, 2, 3))

        def step(state, inp):
            qt, kt, vt, gt = inp
            gate = jnp.exp(gt)
            state = state * gate[..., None] + vt[..., None] * kt[..., None, :]
            out_t = jnp.einsum('bhvk,bhk->bhv', state, qt)
            return (state, out_t)
        state0 = jnp.zeros((Bb, H, Dh, Dh), dtype=x.dtype)
        _, outs = jax.lax.scan(step, state0, (qT, kT, vT, gT))
        out = jnp.transpose(outs, (1, 0, 2, 3)).reshape(Bb, Ll, Hid)
        mu = out.mean(-1, keepdims=True)
        var = out.var(-1, keepdims=True)
        out = (out - mu) / jnp.sqrt(var + 1e-05) * gamma + beta
        out = out * jax.nn.silu(x @ Wg)
        return out @ Wout

    def _L0_ffn_ref(x, w1_w, w1_s, w2_w, w2_s, h1_w, h1_s, h2_w, h2_s, w3_w, w3_s):
        import jax, jax.numpy as jnp
        import numpy as np
        D_IN, D_HID = (128, 512)

        def _ternary(key, shape):
            return jax.random.randint(key, shape, -1, 2).astype(jnp.float32)

        def _tlin(x, w, s):
            return jnp.einsum('bsi,oi->bso', x, w) * s
        h = jax.nn.silu(_tlin(x, w1_w, w1_s)) * _tlin(x, w2_w, w2_s)
        h = jax.nn.gelu(_tlin(h, h1_w, h1_s), approximate=False)
        h = jax.nn.gelu(_tlin(h, h2_w, h2_s), approximate=False)
        return _tlin(h, w3_w, w3_s)
    x = L0_attn_x
    x = _layernorm(x + _L0_attn_ref(x, L0_attn_Wq, L0_attn_Wk, L0_attn_Wv, L0_attn_Wg, L0_attn_Wgk1, L0_attn_Wgk2, L0_attn_bgk2, L0_attn_gamma, L0_attn_beta, L0_attn_Wout), axis=-1)
    x = _layernorm(x + _L0_ffn_ref(x, L0_ffn_w1_w, L0_ffn_w1_s, L0_ffn_w2_w, L0_ffn_w2_s, L0_ffn_h1_w, L0_ffn_h1_s, L0_ffn_h2_w, L0_ffn_h2_s, L0_ffn_w3_w, L0_ffn_w3_s), axis=-1)
    return x

_drawn_inputs = setup_inputs


def setup_inputs(seed=0):
    import zlib

    import numpy as np

    out = dict(_drawn_inputs(seed))
    spreads = {'L0_attn_bgk2': (0.0, 2.0), 'L0_attn_gamma': (1.0, 0.6), 'L0_attn_beta': (0.0, 2.0)}
    factors = {'L0_attn_Wgk1': 64.0,
     'L0_attn_Wgk2': 64.0,
     'L0_ffn_w1_w': 8.0,
     'L0_ffn_w1_s': 8.0,
     'L0_ffn_w2_w': 8.0,
     'L0_ffn_w2_s': 8.0,
     'L0_ffn_h1_w': 8.0,
     'L0_ffn_h1_s': 8.0,
     'L0_ffn_h2_w': 8.0,
     'L0_ffn_h2_s': 8.0,
     'L0_ffn_w3_w': 8.0,
     'L0_ffn_w3_s': 8.0}
    for name, (base, spread) in spreads.items():
        noise = np.random.default_rng([zlib.crc32(name.encode()), seed]).standard_normal(out[name].shape)
        drawn = base * np.exp(spread * noise) if base else spread * noise
        out[name] = jnp.asarray(drawn.astype(out[name].dtype))
    for name, factor in factors.items():
        out[name] = (out[name] * factor).astype(out[name].dtype)
    return out
```

```python
from contextlib import ExitStack

import concourse.bass as bass
from concourse import mybir

P = 128
F32 = mybir.dt.float32
F32R = mybir.dt.float32r
ALU = mybir.AluOpType
ACT = mybir.ActivationFunctionType
EPS = 1e-5
GATE_SCALE = 1.0 / 16.0


def gla_ffn_kernel(nc, x, Wq, Wk, Wv, Wg, Wgk1, Wgk2, bgk2, gamma, beta, Wout,
                   w1_w, w1_s, w2_w, w2_s, h1_w, h1_s, h2_w, h2_s, w3_w, w3_s, out):
    B, L, HID = x.shape
    RANK = Wgk1.shape[1]
    D_HID = w1_w.shape[0]
    HEADS = 16
    DH = HID // HEADS
    TILES = L // P
    OB = D_HID // P
    assert HID == P and L == 512 and DH == 8 and OB == 4

    with ExitStack() as ctx:
        def sb(name, shape, dt=F32):
            return ctx.enter_context(nc.sbuf_tensor(name, shape, dt))

        def sem(name):
            return ctx.enter_context(nc.semaphore(name))

        x_in = sb("x_in", [P, TILES, HID])
        x_res = sb("x_res", [P, TILES, HID])
        proj_raw = sb("proj_raw", [P, 4, HID])
        proj_hi = sb("proj_hi", [P, 5, HID], F32R)
        proj_lo = sb("proj_lo", [P, 5, HID], F32R)
        wgk1 = sb("wgk1", [P, RANK])
        wgk1T = sb("wgk1T", [RANK, HID])
        wgk2 = sb("wgk2", [RANK, HID])
        wout_raw = sb("wout_raw", [P, HID])
        wout_hi = sb("wout_hi", [P, HID], F32R)
        wout_lo = sb("wout_lo", [P, HID], F32R)
        VECS = 4 * OB + 4
        vec_rows = sb("vec_rows", [VECS, P])
        vec_cols = sb("vec_cols", [P, VECS])
        scales = vec_cols[:, 0:4 * OB].rearrange("p (n o) -> p n o", o=OB)
        w3_col, bgk2_col, gamma_col, beta_col = (vec_cols[:, 4 * OB + n:4 * OB + n + 1] for n in range(4))
        w12_raw = sb("w12_raw", [P, 2, OB, HID])
        h_raw = sb("h_raw", [P, 2, OB, D_HID])
        w3_raw = sb("w3_raw", [P, D_HID])
        w12_hi = sb("w12_hi", [P, 2, D_HID], F32R)
        w12_lo = sb("w12_lo", [P, 2, D_HID], F32R)
        h_hi = sb("h_hi", [P, 2, OB, D_HID], F32R)
        h_lo = sb("h_lo", [P, 2, OB, D_HID], F32R)
        w3_hi = sb("w3_hi", [P, OB, HID], F32R)
        w3_lo = sb("w3_lo", [P, OB, HID], F32R)
        ident = sb("ident", [P, P])
        rep_f = sb("rep_f", [P, DH, P])
        rep = sb("rep", [P, DH, P], F32R)
        half_neg = sb("half_neg", [P, TILES])
        eps = sb("eps", [P, TILES])

        x_hi = sb("x_hi", [P, L], F32R)
        x_lo = sb("x_lo", [P, L], F32R)
        kv_tok = sb("kv_tok", [P, TILES, 2 * HID])
        q_hi = sb("q_hi", [P, L], F32R)
        q_lo = sb("q_lo", [P, L], F32R)
        silu_g = sb("silu_g", [P, L])
        z_abs = sb("z_abs", [P, L])
        z_min = sb("z_min", [P, L])
        z_exp = sb("z_exp", [P, L])
        z_ln = sb("z_ln", [P, L])
        z_log = sb("z_log", [P, L])
        gate = sb("gate", [P, L])
        u_tok = sb("u_tok", [P, TILES, DH, P])
        state = sb("state", [P, 2, L])
        y = sb("y", [P, 4, L])
        o_acc = sb("o_acc", [P, L])
        o_stats = sb("o_stats", [P, TILES, 6])
        o_mv = sb("o_mv", [P, TILES, 2])
        o_var = sb("o_var", [P, TILES])
        o_rstd = sb("o_rstd", [P, TILES])
        o_hat = sb("o_hat", [P, TILES, HID])
        og_hi = sb("og_hi", [P, L], F32R)
        og_lo = sb("og_lo", [P, L], F32R)
        r_stats = sb("r_stats", [P, TILES, 6])
        r_mv = sb("r_mv", [P, TILES, 2])
        r_var = sb("r_var", [P, TILES])
        r_rstd = sb("r_rstd", [P, TILES])
        x2 = sb("x2", [P, TILES, HID])
        x2_res = sb("x2_res", [P, B, TILES * HID])
        x2_hi = sb("x2_hi", [P, L], F32R)
        x2_lo = sb("x2_lo", [P, L], F32R)

        silu_a = sb("silu_a", [P, 2, L])
        f1_hi = sb("f1_hi", [P, OB, L], F32R)
        f1_lo = sb("f1_lo", [P, OB, L], F32R)
        f2_hi = sb("f2_hi", [P, OB, L], F32R)
        f2_lo = sb("f2_lo", [P, OB, L], F32R)
        yT = sb("yT", [P, L])
        e_stats = sb("e_stats", [P, TILES, 6])
        e_mv = sb("e_mv", [P, TILES, 2])
        e_var = sb("e_var", [P, TILES])
        e_rstd = sb("e_rstd", [P, TILES])
        out_tok = sb("out_tok", [P, TILES, HID])

        A = [ctx.enter_context(nc.psum_tensor(f"att{i}", [P, L], F32)) for i in range(4)]
        F = [ctx.enter_context(nc.psum_tensor(f"ffn{i}", [P, L], F32)) for i in range(4)]

        x_in_loaded = sem("x_in_loaded")
        x_res_loaded = sem("x_res_loaded")
        proj_loaded = sem("proj_loaded")
        gk_loaded = sem("gk_loaded")
        vecs_loaded = sem("vecs_loaded")
        vecs_turned = sem("vecs_turned")
        vecs_ready = sem("vecs_ready")
        wout_loaded = sem("wout_loaded")
        w12_loaded = sem("w12_loaded")
        h1_loaded = sem("h1_loaded")
        h2_loaded = sem("h2_loaded")
        w3_loaded = sem("w3_loaded")
        consts_zero = sem("consts_zero")
        consts_ready = sem("consts_ready")
        rep_ready = sem("rep_ready")
        proj_hi_ready = sem("proj_hi_ready")
        proj_lo_ready = sem("proj_lo_ready")
        gk1T_ready = sem("gk1T_ready")
        gk1T_copied = sem("gk1T_copied")
        gk12_ready = sem("gk12_ready")
        wout_hi_ready = sem("wout_hi_ready")
        wout_lo_ready = sem("wout_lo_ready")
        wT_ready = sem("wT_ready")
        wT_hi_ready = sem("wT_hi_ready")
        wT_lo_ready = sem("wT_lo_ready")
        xT_ready = sem("xT_ready")
        x_hi_ready = sem("x_hi_ready")
        x_lo_ready = sem("x_lo_ready")
        kv_ready = sem("kv_ready")
        kv_copied = sem("kv_copied")
        z_ready = sem("z_ready")
        q_ready = sem("q_ready")
        g_ready = sem("g_ready")
        q_hi_ready = sem("q_hi_ready")
        q_lo_ready = sem("q_lo_ready")
        silu_g_ready = sem("silu_g_ready")
        z_abs_ready = sem("z_abs_ready")
        z_min_ready = sem("z_min_ready")
        z_exp_ready = sem("z_exp_ready")
        z_ln_ready = sem("z_ln_ready")
        z_log_ready = sem("z_log_ready")
        gate_ready = sem("gate_ready")
        u_ready = sem("u_ready")
        uT_ready = sem("uT_ready")
        q_rep_ready = sem("q_rep_ready")
        scanned = sem("scanned")
        y_ready = sem("y_ready")
        summed = sem("summed")
        oT_ready = sem("oT_ready")
        o_stats_ready = sem("o_stats_ready")
        stats_seen = sem("stats_seen")
        o_mv_ready = sem("o_mv_ready")
        o_var_ready = sem("o_var_ready")
        o_rstd_ready = sem("o_rstd_ready")
        o_hat_ready = sem("o_hat_ready")
        o_hatT_ready = sem("o_hatT_ready")
        affine_done = sem("affine_done")
        gated = sem("gated")
        og_hi_ready = sem("og_hi_ready")
        og_lo_ready = sem("og_lo_ready")
        r_ready = sem("r_ready")
        x1_ready = sem("x1_ready")
        r_stats_ready = sem("r_stats_ready")
        r_mv_ready = sem("r_mv_ready")
        r_var_ready = sem("r_var_ready")
        r_rstd_ready = sem("r_rstd_ready")
        x2_ready = sem("x2_ready")
        x2T_ready = sem("x2T_ready")
        x2_kept = sem("x2_kept")
        x2_hi_ready = sem("x2_hi_ready")
        x2_lo_ready = sem("x2_lo_ready")
        a_ready = sem("a_ready")
        b_ready = sem("b_ready")
        silu_a_ready = sem("silu_a_ready")
        f1_ready = sem("f1_ready")
        f1_hi_ready = sem("f1_hi_ready")
        f1_lo_ready = sem("f1_lo_ready")
        hid_ready = sem("hid_ready")
        gelu_hi_ready = sem("gelu_hi_ready")
        gelu_ready = sem("gelu_ready")
        gelu_lo_ready = sem("gelu_lo_ready")
        w3_ready = sem("w3_ready")
        yT_ready = sem("yT_ready")
        y_tok_ready = sem("y_tok_ready")
        e_sum_ready = sem("e_sum_ready")
        e_stats_ready = sem("e_stats_ready")
        e_mv_ready = sem("e_mv_ready")
        e_var_ready = sem("e_var_ready")
        e_rstd_ready = sem("e_rstd_ready")
        out_ready = sem("out_ready")
        out_stored = sem("out_stored")

        x_rows = x.rearrange("b (j p) c -> b p j c", p=P)
        out_rows = out.rearrange("b (j p) c -> b p j c", p=P)

        def tile(j):
            return slice(j * P, (j + 1) * P)

        weight_banks = []
        for layer in range(2):
            weight_banks.append(([w12_raw[:, layer, o, :] for o in range(OB)],
                                 w12_hi[:, layer, :], w12_lo[:, layer, :], (w12_loaded, 32)))
        for layer, loaded in ((0, h1_loaded), (1, h2_loaded)):
            for c in range(OB):
                weight_banks.append(([h_raw[:, layer, o, tile(c)] for o in range(OB)],
                                     h_hi[:, layer, c, :], h_lo[:, layer, c, :], (loaded, 16)))
        weight_banks.append(([w3_raw[:, tile(c)] for c in range(OB)],
                             w3_hi[:, :, :].rearrange("p c d -> p (c d)"),
                             w3_lo[:, :, :].rearrange("p c d -> p (c d)"), (w3_loaded, 16)))
        WB = len(weight_banks)

        block = ctx.enter_context(nc.Block())

        @block.sync
        def _(sp):
            sp.dma_start(x_in[:], x_rows[0]).then_inc(x_in_loaded, 16)
            for n, w in enumerate((Wk, Wv, Wq, Wg)):
                sp.dma_start(proj_raw[:, n, :], w).then_inc(proj_loaded, 16)
            sp.dma_start(wgk1[:], Wgk1).then_inc(gk_loaded, 16)
            sp.dma_start(wgk2[:], Wgk2).then_inc(gk_loaded, 16)
            for n, v in enumerate((w1_s, w2_s, h1_s, h2_s)):
                sp.dma_start(vec_rows[n * OB:(n + 1) * OB, :],
                             v.rearrange("(o p) -> o p", p=P)).then_inc(vecs_loaded, 16)
            for n, v in enumerate((w3_s, bgk2, gamma, beta)):
                sp.dma_start(vec_rows[4 * OB + n:4 * OB + n + 1, :],
                             v.rearrange("(o p) -> o p", p=P)).then_inc(vecs_loaded, 16)
            for n, w in enumerate((w1_w, w2_w)):
                sp.dma_start(w12_raw[:, n], w.rearrange("(o p) c -> p o c", p=P)).then_inc(w12_loaded, 16)
            sp.dma_start(wout_raw[:], Wout).then_inc(wout_loaded, 16)
            sp.dma_start(x_res[:], x_rows[0]).then_inc(x_res_loaded, 16)
            sp.dma_start(h_raw[:, 0], h1_w.rearrange("(o p) c -> p o c", p=P)).then_inc(h1_loaded, 16)
            sp.dma_start(h_raw[:, 1], h2_w.rearrange("(o p) c -> p o c", p=P)).then_inc(h2_loaded, 16)
            sp.dma_start(w3_raw[:], w3_w).then_inc(w3_loaded, 16)

            def load_x(b):
                sp.wait_ge(xT_ready, b)
                sp.dma_start(x_in[:], x_rows[b]).then_inc(x_in_loaded, 16)

            def load_x_res(b):
                sp.wait_ge(x1_ready, b)
                sp.dma_start(x_res[:], x_rows[b]).then_inc(x_res_loaded, 16)

            def store_out(b):
                sp.wait_ge(out_ready, TILES * (b + 1))
                sp.dma_start(out_rows[b], out_tok[:]).then_inc(out_stored, 16)

            load_x(1)
            load_x_res(1)
            with sp.Fori(0, B - 2) as i:
                load_x(i + 2)
                store_out(i)
                load_x_res(i + 2)
            store_out(B - 2)
            store_out(B - 1)
            sp.wait_ge(out_stored, 16 * B)

        @block.gpsimd
        def _(pool):
            nc.gpsimd.memset(ident[:], 0.0).then_inc(consts_zero, 1)
            nc.gpsimd.memset(rep_f[:], 0.0).then_inc(consts_zero, 1)
            pool.wait_ge(consts_zero, 1)
            nc.gpsimd.affine_select(out=ident[:], in_=ident[:], compare_op=ALU.not_equal, fill=1.0, base=0,
                                    pattern=[[-1, P]], channel_multiplier=1).then_inc(consts_ready, 1)
            pool.wait_ge(consts_zero, 2)
            rep_v = rep_f[:].rearrange("p k (h v) -> p k h v", v=DH)
            nc.gpsimd.affine_select(out=rep_v, in_=rep_v, compare_op=ALU.not_equal, fill=1.0, base=0,
                                    pattern=[[-1, DH], [-DH, HEADS], [0, DH]],
                                    channel_multiplier=1).then_inc(consts_ready, 1)
            nc.gpsimd.memset(half_neg[:], -0.5).then_inc(consts_ready, 1)
            nc.gpsimd.memset(eps[:], EPS).then_inc(consts_ready, 1)
            pool.wait_ge(consts_ready, 4)

            def outer_products(b):
                if not (isinstance(b, int) and b == 0):
                    pool.wait_ge(uT_ready, DH * b)
                for j in range(TILES):
                    pool.wait_ge(kv_copied, 2 * b + j // 2 + 1)
                    k_b = kv_tok[:, j, 0:HID].rearrange("p (h k) -> p k h", k=DH)
                    v_b = kv_tok[:, j, HID:2 * HID].rearrange("p (h v) -> p h v", v=DH)
                    nc.gpsimd.tensor_tensor(
                        u_tok[:, j].rearrange("p k (h v) -> p k h v", v=DH),
                        v_b.unsqueeze(1).to_broadcast([P, DH, HEADS, DH]),
                        k_b.unsqueeze(3).to_broadcast([P, DH, HEADS, DH]), ALU.mult).then_inc(u_ready, 1)

            def log_gate(b):
                pool.wait_ge(z_ln_ready, b + 1)
                pool.wait_ge(z_min_ready, b + 1)
                nc.gpsimd.tensor_tensor(z_log[:], z_min[:], z_ln[:], ALU.subtract).then_inc(z_log_ready, 1)

            def sum_over_k(b):
                for k in range(1, DH):
                    pool.wait_ge(y_ready, DH * b + k + 1)
                    if k == 1:
                        if not (isinstance(b, int) and b == 0):
                            pool.wait_ge(oT_ready, b)
                        first = y[:, 0]
                    else:
                        pool.wait_ge(summed, (DH - 1) * b + k - 1)
                        first = o_acc[:]
                    nc.gpsimd.tensor_tensor(o_acc[:], first, y[:, k % 4], ALU.add).then_inc(summed, 1)

            def rstd_of(b, mv_ready, mv, var, var_ready, rstd, rstd_ready):
                pool.wait_ge(mv_ready, TILES * (b + 1))
                nc.gpsimd.tensor_tensor(var[:], mv[:, :, 1], eps[:], ALU.add).then_inc(var_ready, 1)
                pool.wait_ge(var_ready, b + 1)
                nc.gpsimd.tensor_tensor(rstd[:], var[:], half_neg[:], ALU.pow).then_inc(rstd_ready, 1)

            def o_rstd_of(b):
                rstd_of(b, o_mv_ready, o_mv, o_var, o_var_ready, o_rstd, o_rstd_ready)

            def r_rstd_of(b):
                rstd_of(b, r_mv_ready, r_mv, r_var, r_var_ready, r_rstd, r_rstd_ready)

            def e_rstd_of(b):
                rstd_of(b, e_mv_ready, e_mv, e_var, e_var_ready, e_rstd, e_rstd_ready)

            def attention(b):
                outer_products(b)
                log_gate(b)
                sum_over_k(b)
                o_rstd_of(b)
                r_rstd_of(b)

            attention(0)
            with pool.Fori(0, B - 1) as i:
                attention(i + 1)
                e_rstd_of(i)
            e_rstd_of(B - 1)

        @block.tensor
        def _(pe):
            def three_passes(ps, wh, wl, mh, ml, start=True, stop=True, before_lo=None):
                nc.tensor.matmul(ps, wh, mh, start=start, stop=False)
                nc.tensor.matmul(ps, wl, mh, start=False, stop=False)
                if before_lo is not None:
                    pe.wait_ge(*before_lo)
                return nc.tensor.matmul(ps, wh, ml, start=False, stop=stop)

            def transpose_x(b):
                pe.wait_ge(x_in_loaded, 16 * (b + 1))
                for j in range(TILES):
                    last = nc.tensor.transpose(A[0][:, tile(j)], x_in[:, j, :], ident[:])
                last.then_inc(xT_ready, 1)

            def project(b):
                pe.wait_ge(x_hi_ready, b + 1)
                pe.wait_ge(x_lo_ready, b + 1)
                if not (isinstance(b, int) and b == 0):
                    pe.wait_ge(x2_lo_ready, b)
                kv_h = proj_hi[:, 0:2, :].rearrange("p n c -> p (n c)")
                kv_l = proj_lo[:, 0:2, :].rearrange("p n c -> p (n c)")
                for pair in range(2):
                    for half in range(2):
                        t = tile(2 * pair + half)
                        ps = A[1 + pair][:, half * 2 * HID:(half + 1) * 2 * HID]
                        nc.tensor.matmul(ps, x_hi[:, t], kv_h, start=True, stop=False)
                        nc.tensor.matmul(ps, x_hi[:, t], kv_l, start=False, stop=False)
                        last = nc.tensor.matmul(ps, x_lo[:, t], kv_h, start=False, stop=True)
                    last.then_inc(kv_ready, 1)
                if isinstance(b, int) and b == 0:
                    pe.wait_ge(proj_lo_ready, 2)
                three_passes(A[3][:], proj_hi[:, 4], proj_lo[:, 4], x_hi[:], x_lo[:]).then_inc(z_ready, 1)
                three_passes(A[0][:], proj_hi[:, 2], proj_lo[:, 2], x_hi[:], x_lo[:]).then_inc(q_ready, 1)
                pe.wait_ge(kv_copied, 2 * b + 1)
                three_passes(A[1][:], proj_hi[:, 3], proj_lo[:, 3], x_hi[:], x_lo[:]).then_inc(g_ready, 1)

            def replicate_q(b, k):
                if k == 0:
                    pe.wait_ge(q_hi_ready, b + 1)
                    pe.wait_ge(q_lo_ready, b + 1)
                elif k == 1:
                    pe.wait_ge(silu_g_ready, b + 1)
                else:
                    pe.wait_ge(y_ready, DH * b + k - 1)
                nc.tensor.matmul(A[k % 2][:], rep[:, k], q_hi[:], start=True, stop=False)
                nc.tensor.matmul(A[k % 2][:], rep[:, k], q_lo[:], start=False, stop=True).then_inc(q_rep_ready, 1)

            def transpose_u(b, k):
                if k == 0:
                    pe.wait_ge(u_ready, TILES * (b + 1))
                elif k == 1:
                    pe.wait_ge(z_abs_ready, b + 1)
                    pe.wait_ge(z_min_ready, b + 1)
                else:
                    pe.wait_ge(scanned, DH * b + k - 1)
                for j in range(TILES):
                    last = nc.tensor.transpose(A[2 + k % 2][:, tile(j)], u_tok[:, j, k], ident[:])
                last.then_inc(uT_ready, 1)

            def transpose_o(b):
                pe.wait_ge(summed, (DH - 1) * (b + 1))
                for j in range(TILES):
                    last = nc.tensor.transpose(A[2][:, tile(j)], o_acc[:, tile(j)], ident[:])
                last.then_inc(oT_ready, 1)

            def transpose_o_hat(b):
                pe.wait_ge(o_hat_ready, TILES * (b + 1))
                for j in range(TILES):
                    last = nc.tensor.transpose(A[3][:, tile(j)], o_hat[:, j], ident[:])
                last.then_inc(o_hatT_ready, 1)

            def project_out(b):
                pe.wait_ge(og_hi_ready, b + 1)
                pe.wait_ge(og_lo_ready, b + 1)
                for j in range(TILES):
                    ps = A[0][:, tile(j)]
                    nc.tensor.matmul(ps, og_hi[:, tile(j)], wout_hi[:], start=True, stop=False)
                    nc.tensor.matmul(ps, og_hi[:, tile(j)], wout_lo[:], start=False, stop=False)
                    last = nc.tensor.matmul(ps, og_lo[:, tile(j)], wout_hi[:], start=False, stop=True)
                last.then_inc(r_ready, 1)

            def transpose_x2(b):
                pe.wait_ge(x2_ready, TILES * (b + 1))
                for j in range(TILES):
                    last = nc.tensor.transpose(A[1][:, tile(j)], x2[:, j], ident[:])
                last.then_inc(x2T_ready, 1)

            def ffn_in(b, o):
                if o == 0:
                    pe.wait_ge(x2_hi_ready, b + 1)
                    pe.wait_ge(x2_lo_ready, b + 1)
                    if not (isinstance(b, int) and b == 0):
                        pe.wait_ge(out_ready, TILES * b)
                if o >= 2:
                    pe.wait_ge(silu_a_ready, OB * b + o - 1)
                fa, fb = F[(2 * o) % 4], F[(2 * o + 1) % 4]
                three_passes(fa[:], w12_hi[:, 0, tile(o)], w12_lo[:, 0, tile(o)],
                             x2_hi[:], x2_lo[:]).then_inc(a_ready, 1)
                if o >= 2:
                    pe.wait_ge(f1_lo_ready, OB * b + o - 1)
                three_passes(fb[:], w12_hi[:, 1, tile(o)], w12_lo[:, 1, tile(o)],
                             x2_hi[:], x2_lo[:]).then_inc(b_ready, 1)

            def ffn_hidden(b, layer, o):
                src_hi, src_lo = ((f1_hi, f1_lo), (f2_hi, f2_lo))[layer]
                if layer == 0:
                    if o in (0, 2):
                        pe.wait_ge(silu_a_ready, OB * b + OB - 1 + o // 2)
                    else:
                        pe.wait_ge(f1_lo_ready, OB * b + OB - 1 + o // 2)
                else:
                    pe.wait_ge(gelu_lo_ready, 2 * OB * b + o + 1)
                for c in range(OB):
                    if layer == 0:
                        pe.wait_ge(f1_hi_ready, OB * b + c + 1)
                    else:
                        pe.wait_ge(gelu_hi_ready, 2 * OB * b + c + 1)
                    nc.tensor.matmul(F[o][:], h_hi[:, layer, c, tile(o)], src_hi[:, c], start=(c == 0), stop=False)
                    nc.tensor.matmul(F[o][:], h_lo[:, layer, c, tile(o)], src_hi[:, c], start=False, stop=False)
                for c in range(OB):
                    if layer == 0:
                        pe.wait_ge(f1_lo_ready, OB * b + c + 1)
                    else:
                        pe.wait_ge(gelu_lo_ready, 2 * OB * b + c + 1)
                    last = nc.tensor.matmul(F[o][:], h_hi[:, layer, c, tile(o)], src_lo[:, c],
                                            start=False, stop=(c == OB - 1))
                last.then_inc(hid_ready, 1)

            def ffn_out(b):
                for c in range(OB):
                    pe.wait_ge(gelu_hi_ready, 2 * OB * b + OB + c + 1)
                    if c == 0:
                        pe.wait_ge(gelu_lo_ready, 2 * OB * b + OB + 1)
                    nc.tensor.matmul(F[0][:], w3_hi[:, c], f1_hi[:, c], start=(c == 0), stop=False)
                    nc.tensor.matmul(F[0][:], w3_lo[:, c], f1_hi[:, c], start=False, stop=False)
                for c in range(OB):
                    pe.wait_ge(gelu_lo_ready, 2 * OB * b + OB + c + 1)
                    last = nc.tensor.matmul(F[0][:], w3_hi[:, c], f1_lo[:, c], start=False, stop=(c == OB - 1))
                last.then_inc(w3_ready, 1)

            def transpose_y(b):
                pe.wait_ge(yT_ready, b + 1)
                for j in range(TILES):
                    last = nc.tensor.transpose(F[1][:, tile(j)], yT[:, tile(j)], ident[:])
                last.then_inc(y_tok_ready, 1)

            def weight_bank(n):
                blocks, _, _, loaded = weight_banks[n]
                pe.wait_ge(*loaded)
                if n >= 4:
                    pe.wait_ge(wT_lo_ready, n - 3)
                for j, w in enumerate(blocks):
                    last = nc.tensor.transpose(F[n % 4][:, tile(j)], w, ident[:])
                last.then_inc(wT_ready, 1)

            pe.wait_ge(consts_ready, 1)
            transpose_x(0)
            pe.wait_ge(gk_loaded, 32)
            nc.tensor.transpose(A[3][0:RANK, 0:P], wgk1[:], ident[:]).then_inc(gk1T_ready, 1)
            pe.wait_ge(gk1T_copied, 1)
            nc.tensor.matmul(A[3][:, P:2 * P], wgk1T[:], wgk2[:], start=True, stop=True).then_inc(gk12_ready, 1)
            pe.wait_ge(vecs_loaded, 16 * 8)
            nc.tensor.transpose(A[1][:, 0:VECS], vec_rows[:],
                                ident[0:VECS, 0:VECS]).then_inc(vecs_turned, 1)
            pe.wait_ge(vecs_ready, 1)
            pe.wait_ge(proj_hi_ready, 1)
            pe.wait_ge(proj_lo_ready, 1)
            project(0)
            pe.wait_ge(rep_ready, 1)
            replicate_q(0, 0)
            replicate_q(0, 1)
            for n in range(WB):
                weight_bank(n)
            for k in range(DH):
                transpose_u(0, k)
                if k >= 2:
                    replicate_q(0, k)
            transpose_o(0)
            transpose_o_hat(0)
            pe.wait_ge(wout_hi_ready, 1)
            pe.wait_ge(wout_lo_ready, 1)
            project_out(0)
            transpose_x2(0)
            pe.wait_ge(wT_lo_ready, WB)

            with pe.Fori(0, B - 1) as i:
                a, f = i + 1, i
                transpose_x(a)
                ffn_in(f, 0)
                project(a)
                ffn_in(f, 1)
                ffn_in(f, 2)
                replicate_q(a, 0)
                ffn_in(f, 3)
                replicate_q(a, 1)
                ffn_hidden(f, 0, 0)
                transpose_u(a, 0)
                transpose_u(a, 1)
                ffn_hidden(f, 0, 1)
                transpose_u(a, 2)
                replicate_q(a, 2)
                ffn_hidden(f, 0, 2)
                transpose_u(a, 3)
                replicate_q(a, 3)
                ffn_hidden(f, 0, 3)
                transpose_u(a, 4)
                replicate_q(a, 4)
                transpose_u(a, 5)
                ffn_hidden(f, 1, 0)
                replicate_q(a, 5)
                transpose_u(a, 6)
                replicate_q(a, 6)
                ffn_hidden(f, 1, 1)
                transpose_u(a, 7)
                replicate_q(a, 7)
                ffn_hidden(f, 1, 2)
                transpose_o(a)
                ffn_hidden(f, 1, 3)
                transpose_o_hat(a)
                ffn_out(f)
                project_out(a)
                transpose_y(f)
                transpose_x2(a)

            last_row = B - 1
            for o in range(OB):
                ffn_in(last_row, o)
            for layer in range(2):
                for o in range(OB):
                    ffn_hidden(last_row, layer, o)
            ffn_out(last_row)
            transpose_y(last_row)

        @block.scalar
        def _(act):
            def round_x(b):
                act.wait_ge(xT_ready, b + 1)
                nc.scalar.copy(x_hi[:], A[0][:]).then_inc(x_hi_ready, 1)

            def copy_kv(b):
                if not (isinstance(b, int) and b == 0):
                    act.wait_ge(u_ready, TILES * b)
                for pair in range(2):
                    act.wait_ge(kv_ready, 2 * b + pair + 1)
                    nc.scalar.copy(kv_tok[:, 2 * pair:2 * pair + 2, :].rearrange("p j c -> p (j c)"),
                                   A[1 + pair][:]).then_inc(kv_copied, 1)

            def gates(b):
                act.wait_ge(z_ready, b + 1)
                nc.scalar.activation(z_abs[:], A[3][:], ACT.Abs, bias=bgk2_col).then_inc(z_abs_ready, 1)
                act.wait_ge(z_abs_ready, b + 1)
                nc.scalar.activation(z_exp[:], z_abs[:], ACT.Exp, scale=-1.0).then_inc(z_exp_ready, 1)
                act.wait_ge(z_exp_ready, b + 1)
                nc.scalar.activation(z_ln[:], z_exp[:], ACT.Ln, bias=1.0).then_inc(z_ln_ready, 1)
                act.wait_ge(z_log_ready, b + 1)
                if not (isinstance(b, int) and b == 0):
                    act.wait_ge(scanned, DH * b)
                nc.scalar.activation(gate[:], z_log[:], ACT.Exp, scale=GATE_SCALE).then_inc(gate_ready, 1)

            def round_q(b):
                act.wait_ge(q_ready, b + 1)
                if not (isinstance(b, int) and b == 0):
                    act.wait_ge(q_rep_ready, DH * b)
                nc.scalar.copy(q_hi[:], A[0][:]).then_inc(q_hi_ready, 1)

            def silu_of_g(b):
                act.wait_ge(g_ready, b + 1)
                if not (isinstance(b, int) and b == 0):
                    act.wait_ge(gated, b)
                nc.scalar.activation(silu_g[:], A[1][:], ACT.Silu).then_inc(silu_g_ready, 1)

            def affine(b):
                act.wait_ge(o_hatT_ready, b + 1)
                nc.scalar.activation(A[3][:], A[3][:], ACT.Identity, scale=gamma_col,
                                     bias=beta_col).then_inc(affine_done, 1)

            def round_og(b):
                act.wait_ge(gated, b + 1)
                if not (isinstance(b, int) and b == 0):
                    act.wait_ge(r_ready, b)
                nc.scalar.copy(og_hi[:], A[3][:]).then_inc(og_hi_ready, 1)

            def keep_x2(b):
                act.wait_ge(x2_ready, TILES * (b + 1))
                nc.scalar.copy(x2_res[:, b, :], x2[:].rearrange("p j c -> p (j c)")).then_inc(x2_kept, 1)

            def round_x2(b):
                act.wait_ge(x2T_ready, b + 1)
                if not (isinstance(b, int) and b == 0):
                    act.wait_ge(b_ready, OB * b)
                nc.scalar.copy(x2_hi[:], A[1][:]).then_inc(x2_hi_ready, 1)

            def ffn_silu(b, o):
                act.wait_ge(a_ready, OB * b + o + 1)
                if o >= 2:
                    act.wait_ge(f1_ready, OB * b + o - 1)
                elif not (isinstance(b, int) and b == 0):
                    act.wait_ge(f1_ready, OB * b)
                nc.scalar.activation(silu_a[:, o % 2], F[(2 * o) % 4][:], ACT.Silu,
                                     scale=scales[:, 0, o:o + 1]).then_inc(silu_a_ready, 1)

            def ffn_round(b, o):
                act.wait_ge(f1_ready, OB * b + o + 1)
                if o == 0 and not (isinstance(b, int) and b == 0):
                    act.wait_ge(w3_ready, b)
                nc.scalar.copy(f1_hi[:, o], F[(2 * o + 1) % 4][:]).then_inc(f1_hi_ready, 1)

            def ffn_gelu(b, layer, o):
                dst = (f2_hi, f1_hi)[layer]
                n = 2 * OB * b + OB * layer + o + 1
                if layer == 0:
                    if o == 0 and not (isinstance(b, int) and b == 0):
                        act.wait_ge(hid_ready, 2 * OB * b)
                elif o == 0:
                    act.wait_ge(hid_ready, 2 * OB * b + OB)
                act.wait_ge(hid_ready, n)
                nc.scalar.activation(dst[:, o], F[o][:], ACT.Gelu,
                                     scale=scales[:, 2 + layer, o:o + 1]).then_inc(gelu_hi_ready, 1)
                act.wait_ge(gelu_hi_ready, n)
                nc.scalar.activation(F[o][:], F[o][:], ACT.Gelu,
                                     scale=scales[:, 2 + layer, o:o + 1]).then_inc(gelu_ready, 1)

            def scale_y(b):
                act.wait_ge(w3_ready, b + 1)
                if not (isinstance(b, int) and b == 0):
                    act.wait_ge(y_tok_ready, b)
                nc.scalar.activation(yT[:], F[0][:], ACT.Identity, scale=w3_col).then_inc(yT_ready, 1)

            def weight_bank_hi(n):
                act.wait_ge(wT_ready, n + 1)
                nc.scalar.copy(weight_banks[n][1], F[n % 4][:]).then_inc(wT_hi_ready, 1)

            round_x(0)
            act.wait_ge(proj_loaded, 64)
            nc.scalar.copy(proj_hi[:, 0:4], proj_raw[:]).then_inc(proj_hi_ready, 1)
            act.wait_ge(gk1T_ready, 1)
            nc.scalar.copy(wgk1T[:], A[3][0:RANK, 0:P]).then_inc(gk1T_copied, 1)
            act.wait_ge(gk12_ready, 1)
            nc.scalar.copy(proj_hi[:, 4], A[3][:, P:2 * P]).then_inc(proj_hi_ready, 1)
            act.wait_ge(vecs_turned, 1)
            nc.scalar.copy(vec_cols[:], A[1][:, 0:VECS]).then_inc(vecs_ready, 1)
            copy_kv(0)
            act.wait_ge(consts_ready, 2)
            nc.scalar.copy(rep[:], rep_f[:]).then_inc(rep_ready, 1)
            round_q(0)
            gates(0)
            silu_of_g(0)
            act.wait_ge(wout_loaded, 16)
            nc.scalar.copy(wout_hi[:], wout_raw[:]).then_inc(wout_hi_ready, 1)
            for n in range(WB):
                weight_bank_hi(n)
            act.wait_ge(vecs_ready, 1)
            affine(0)
            round_og(0)
            keep_x2(0)
            round_x2(0)

            with act.Fori(0, B - 1) as i:
                a, f = i + 1, i
                round_x(a)
                copy_kv(a)
                round_q(a)
                gates(a)
                silu_of_g(a)
                for o in range(OB):
                    ffn_silu(f, o)
                    if o >= 1:
                        ffn_round(f, o - 1)
                ffn_round(f, OB - 1)
                for o in range(OB):
                    ffn_gelu(f, 0, o)
                for o in range(OB):
                    ffn_gelu(f, 1, o)
                affine(a)
                round_og(a)
                scale_y(f)
                keep_x2(a)
                round_x2(a)

            last_row = B - 1
            for o in range(OB):
                ffn_silu(last_row, o)
                if o >= 1:
                    ffn_round(last_row, o - 1)
            ffn_round(last_row, OB - 1)
            for layer in range(2):
                for o in range(OB):
                    ffn_gelu(last_row, layer, o)
            scale_y(last_row)

        @block.vector
        def _(dve):
            def rest_of_x(b):
                dve.wait_ge(x_hi_ready, b + 1)
                nc.vector.tensor_tensor(x_lo[:], A[0][:], x_hi[:].bitcast(F32), ALU.subtract).then_inc(x_lo_ready, 1)

            def read_z(b):
                dve.wait_ge(z_ready, b + 1)
                dve.wait_ge(z_abs_ready, b + 1)
                nc.vector.tensor_scalar(z_min[:], A[3][:], bgk2_col, 0.0, ALU.add,
                                        ALU.min).then_inc(z_min_ready, 1)

            def rest_of_q(b):
                dve.wait_ge(q_hi_ready, b + 1)
                nc.vector.tensor_tensor(q_lo[:], A[0][:], q_hi[:].bitcast(F32), ALU.subtract).then_inc(q_lo_ready, 1)

            def scan(b, k):
                dve.wait_ge(uT_ready, DH * b + k + 1)
                if k == 0:
                    dve.wait_ge(gate_ready, b + 1)
                if k >= 2:
                    dve.wait_ge(y_ready, DH * b + k - 1)
                elif not (isinstance(b, int) and b == 0):
                    dve.wait_ge(y_ready, DH * b)
                nc.vector.tensor_tensor_scan(state[:, k % 2], gate[:], A[2 + k % 2][:], 0.0,
                                             ALU.mult, ALU.add).then_inc(scanned, 1)

            def read_out(b, k):
                dve.wait_ge(q_rep_ready, DH * b + k + 1)
                dve.wait_ge(scanned, DH * b + k + 1)
                if k >= 4:
                    dve.wait_ge(summed, (DH - 1) * b + max(k - 4, 1))
                elif not (isinstance(b, int) and b == 0):
                    dve.wait_ge(summed, (DH - 1) * b)
                nc.vector.tensor_tensor(y[:, k % 4], A[k % 2][:], state[:, k % 2], ALU.mult).then_inc(y_ready, 1)

            def statistics(b, bank, stats, stats_ready, mv, mv_ready):
                for j in range(TILES):
                    nc.vector.bn_stats(stats[:, j], bank[:, tile(j)]).then_inc(stats_ready, 1)
                for j in range(TILES):
                    if j == 0:
                        dve.wait_ge(stats_ready, TILES * (b + 1))
                        dve.sem_inc(stats_seen, 1)
                    nc.vector.bn_aggr(mv[:, j], stats[:, j]).then_inc(mv_ready, 1)

            def normalise(dst, dst_ready, bank, mv, rstd):
                for j in range(TILES):
                    nc.vector.tensor_scalar(dst[:, j], bank[:, tile(j)], mv[:, j, 0:1], rstd[:, j:j + 1],
                                            ALU.subtract, ALU.mult).then_inc(dst_ready, 1)

            def o_statistics(b):
                dve.wait_ge(oT_ready, b + 1)
                statistics(b, A[2], o_stats, o_stats_ready, o_mv, o_mv_ready)

            def o_normalise(b):
                dve.wait_ge(o_rstd_ready, b + 1)
                normalise(o_hat, o_hat_ready, A[2], o_mv, o_rstd)

            def apply_gate(b):
                dve.wait_ge(affine_done, b + 1)
                dve.wait_ge(silu_g_ready, b + 1)
                nc.vector.tensor_tensor(A[3][:], A[3][:], silu_g[:], ALU.mult).then_inc(gated, 1)

            def rest_of_og(b):
                dve.wait_ge(og_hi_ready, b + 1)
                nc.vector.tensor_tensor(og_lo[:], A[3][:], og_hi[:].bitcast(F32), ALU.subtract).then_inc(og_lo_ready, 1)

            def add_x(b):
                dve.wait_ge(r_ready, b + 1)
                dve.wait_ge(x_res_loaded, 16 * (b + 1))
                nc.vector.tensor_tensor(A[0][:], A[0][:], x_res[:].rearrange("p j c -> p (j c)"),
                                        ALU.add).then_inc(x1_ready, 1)
                dve.wait_ge(x1_ready, b + 1)
                statistics(b, A[0], r_stats, r_stats_ready, r_mv, r_mv_ready)

            def x2_normalise(b):
                dve.wait_ge(r_rstd_ready, b + 1)
                if not (isinstance(b, int) and b == 0):
                    dve.wait_ge(x2T_ready, b)
                    dve.wait_ge(x2_kept, b)
                normalise(x2, x2_ready, A[0], r_mv, r_rstd)

            def rest_of_x2(b):
                dve.wait_ge(x2_hi_ready, b + 1)
                nc.vector.tensor_tensor(x2_lo[:], A[1][:], x2_hi[:].bitcast(F32), ALU.subtract).then_inc(x2_lo_ready, 1)

            def ffn_product(b, o):
                bank = F[(2 * o + 1) % 4]
                dve.wait_ge(b_ready, OB * b + o + 1)
                dve.wait_ge(silu_a_ready, OB * b + o + 1)
                nc.vector.scalar_tensor_tensor(bank[:], bank[:], scales[:, 1, o:o + 1], silu_a[:, o % 2],
                                               ALU.mult, ALU.mult).then_inc(f1_ready, 1)

            def ffn_rest(b, o):
                dve.wait_ge(f1_hi_ready, OB * b + o + 1)
                nc.vector.tensor_tensor(f1_lo[:, o], F[(2 * o + 1) % 4][:], f1_hi[:, o].bitcast(F32),
                                        ALU.subtract).then_inc(f1_lo_ready, 1)

            def gelu_rest(b, layer, o):
                hi, lo = ((f2_hi, f2_lo), (f1_hi, f1_lo))[layer]
                dve.wait_ge(gelu_ready, 2 * OB * b + OB * layer + o + 1)
                nc.vector.tensor_tensor(lo[:, o], F[o][:], hi[:, o].bitcast(F32),
                                        ALU.subtract).then_inc(gelu_lo_ready, 1)

            def add_x2(b):
                dve.wait_ge(y_tok_ready, b + 1)
                dve.wait_ge(x2_kept, b + 1)
                nc.vector.tensor_tensor(F[1][:], F[1][:], x2_res[:, b, :], ALU.add).then_inc(e_sum_ready, 1)
                dve.wait_ge(e_sum_ready, b + 1)
                statistics(b, F[1], e_stats, e_stats_ready, e_mv, e_mv_ready)

            def out_normalise(b):
                dve.wait_ge(e_rstd_ready, b + 1)
                if not (isinstance(b, int) and b == 0):
                    dve.wait_ge(out_stored, 16 * b)
                normalise(out_tok, out_ready, F[1], e_mv, e_rstd)

            def weight_bank_lo(n):
                dve.wait_ge(wT_hi_ready, n + 1)
                _, hi, lo, _ = weight_banks[n]
                nc.vector.tensor_tensor(lo, F[n % 4][:], hi.bitcast(F32), ALU.subtract).then_inc(wT_lo_ready, 1)

            rest_of_x(0)
            dve.wait_ge(proj_hi_ready, 1)
            nc.vector.tensor_tensor(proj_lo[:, 0:4], proj_raw[:], proj_hi[:, 0:4].bitcast(F32),
                                    ALU.subtract).then_inc(proj_lo_ready, 1)
            dve.wait_ge(proj_hi_ready, 2)
            nc.vector.tensor_tensor(proj_lo[:, 4], A[3][:, P:2 * P], proj_hi[:, 4].bitcast(F32),
                                    ALU.subtract).then_inc(proj_lo_ready, 1)
            dve.wait_ge(vecs_ready, 1)
            read_z(0)
            rest_of_q(0)
            dve.wait_ge(wout_hi_ready, 1)
            nc.vector.tensor_tensor(wout_lo[:], wout_raw[:], wout_hi[:].bitcast(F32),
                                    ALU.subtract).then_inc(wout_lo_ready, 1)
            for n in range(WB):
                weight_bank_lo(n)
            scan(0, 0)
            for k in range(1, DH):
                scan(0, k)
                read_out(0, k - 1)
            read_out(0, DH - 1)
            o_statistics(0)
            o_normalise(0)
            apply_gate(0)
            rest_of_og(0)
            add_x(0)
            x2_normalise(0)
            rest_of_x2(0)

            with dve.Fori(0, B - 1) as i:
                a, f = i + 1, i
                rest_of_x(a)
                read_z(a)
                rest_of_q(a)
                for o in range(OB):
                    ffn_product(f, o)
                    ffn_rest(f, o)
                scan(a, 0)
                scan(a, 1)
                read_out(a, 0)
                gelu_rest(f, 0, 0)
                scan(a, 2)
                read_out(a, 1)
                gelu_rest(f, 0, 1)
                scan(a, 3)
                read_out(a, 2)
                gelu_rest(f, 0, 2)
                scan(a, 4)
                read_out(a, 3)
                gelu_rest(f, 0, 3)
                scan(a, 5)
                read_out(a, 4)
                gelu_rest(f, 1, 0)
                scan(a, 6)
                read_out(a, 5)
                gelu_rest(f, 1, 1)
                scan(a, 7)
                read_out(a, 6)
                read_out(a, 7)
                gelu_rest(f, 1, 2)
                o_statistics(a)
                gelu_rest(f, 1, 3)
                o_normalise(a)
                apply_gate(a)
                rest_of_og(a)
                add_x(a)
                x2_normalise(a)
                add_x2(f)
                rest_of_x2(a)
                out_normalise(f)

            last_row = B - 1
            for o in range(OB):
                ffn_product(last_row, o)
                ffn_rest(last_row, o)
            for layer in range(2):
                for o in range(OB):
                    gelu_rest(last_row, layer, o)
            add_x2(last_row)
            out_normalise(last_row)


_INS = ['L0_attn_x', 'L0_attn_Wq', 'L0_attn_Wk', 'L0_attn_Wv', 'L0_attn_Wg', 'L0_attn_Wgk1', 'L0_attn_Wgk2',
        'L0_attn_bgk2', 'L0_attn_gamma', 'L0_attn_beta', 'L0_attn_Wout', 'L0_ffn_w1_w', 'L0_ffn_w1_s',
        'L0_ffn_w2_w', 'L0_ffn_w2_s', 'L0_ffn_h1_w', 'L0_ffn_h1_s', 'L0_ffn_h2_w', 'L0_ffn_h2_s',
        'L0_ffn_w3_w', 'L0_ffn_w3_s']


def kernel(**inputs):
    import numpy as np
    import concourse.bacc as bacc
    from concourse.bass_utils import run_bass_kernel_spmd

    nc = bacc.Bacc("TRN2", target_bir_lowering=False, num_devices=1)
    arrays, args = {}, []
    for name in _INS:
        a = np.ascontiguousarray(inputs[name])
        arrays[f"in_{name}"] = a
        args.append(nc.dram_tensor(f"in_{name}", a.shape, mybir.dt.from_np(a.dtype), kind="ExternalInput").ap())
    out = nc.dram_tensor("out_0", inputs['L0_attn_x'].shape, F32, kind="ExternalOutput").ap()
    gla_ffn_kernel(nc, *args, out)
    r = run_bass_kernel_spmd(nc, [arrays], core_ids=[0])
    return r.results[0]["out_0"]
```

```python
from contextlib import ExitStack

import concourse.bass as bass
from concourse import mybir

P = 128
F32 = mybir.dt.float32
F32R = mybir.dt.float32r
ALU = mybir.AluOpType
ACT = mybir.ActivationFunctionType
EPS = 1e-5
GATE_SCALE = 1.0 / 16.0


def gla_ffn_kernel(nc, x, Wq, Wk, Wv, Wg, Wgk1, Wgk2, bgk2, gamma, beta, Wout,
                   w1_w, w1_s, w2_w, w2_s, h1_w, h1_s, h2_w, h2_s, w3_w, w3_s, out):
    B, L, HID = x.shape
    RANK = Wgk1.shape[1]
    D_HID = w1_w.shape[0]
    HEADS = 16
    DH = HID // HEADS
    TILES = L // P
    OB = D_HID // P
    assert HID == P and L == 512 and DH == 8 and OB == 4

    with ExitStack() as ctx:
        def sb(name, shape, dt=F32):
            return ctx.enter_context(nc.sbuf_tensor(name, shape, dt))

        def sem(name):
            return ctx.enter_context(nc.semaphore(name))

        def arena(name, nbytes, *tensors):
            base = -(-nc.sbuf_base // 32) * 32
            slab = sb(name, [P, nbytes // 4])
            return [nc.alloc_sbuf_tensor_at(n, shape, dt, offset=base + off) for n, shape, dt, off in tensors]

        ROW = L * 4
        x_hi, x_lo, f1_hi, f1_lo = arena(
            "place_f1", 2 * B * ROW, ("x_hi", [P, B, L], F32R, 0), ("x_lo", [P, B, L], F32R, B * ROW),
            ("f1_hi", [P, OB, L], F32R, 0), ("f1_lo", [P, OB, L], F32R, OB * ROW))
        h_raw, f2_hi, f2_lo = arena(
            "place_f2", 2 * OB * ROW, ("h_raw", [P, 2, OB, D_HID], F32, 0),
            ("f2_hi", [P, OB, L], F32R, 0), ("f2_lo", [P, OB, L], F32R, OB * ROW))
        w12_raw, w3_raw, out_tok = arena(
            "place_out", B * ROW, ("w12_raw", [P, 2, OB, HID], F32, 0), ("w3_raw", [P, D_HID], F32, 2 * ROW),
            ("out_tok", [P, B, TILES, HID], F32, 0))
        rep_f, y = arena(
            "place_y", 4 * ROW, ("rep_f", [P, DH, P], F32, 0), ("y", [P, 4, L], F32, 0))

        x_tok = sb("x_tok", [P, B, TILES, HID])
        proj_raw = sb("proj_raw", [P, 4, HID])
        proj_hi = sb("proj_hi", [P, 5, HID], F32R)
        proj_lo = sb("proj_lo", [P, 5, HID], F32R)
        wgk1 = sb("wgk1", [P, RANK])
        wgk1T = sb("wgk1T", [RANK, HID])
        wgk2 = sb("wgk2", [RANK, HID])
        wout = sb("wout", [P, HID])
        VECS = 4 * OB + 4
        vec_rows = sb("vec_rows", [VECS, P])
        vec_cols = sb("vec_cols", [P, VECS])
        scales = vec_cols[:, 0:4 * OB].rearrange("p (n o) -> p n o", o=OB)
        w3_col, bgk2_col, gamma_col, beta_col = (vec_cols[:, 4 * OB + n:4 * OB + n + 1] for n in range(4))
        w12_hi = sb("w12_hi", [P, 2, D_HID], F32R)
        w12_lo = sb("w12_lo", [P, 2, D_HID], F32R)
        h_hi = sb("h_hi", [P, 2, OB, D_HID], F32R)
        h_lo = sb("h_lo", [P, 2, OB, D_HID], F32R)
        w3_hi = sb("w3_hi", [P, OB, HID], F32R)
        w3_lo = sb("w3_lo", [P, OB, HID], F32R)
        ident = sb("ident", [P, P])
        rep = sb("rep", [P, DH, P], F32R)
        half_neg = sb("half_neg", [P, TILES])
        eps = sb("eps", [P, TILES])

        kv_tok = sb("kv_tok", [P, B, TILES, 2 * HID])
        q_hi = sb("q_hi", [P, B, L], F32R)
        q_lo = sb("q_lo", [P, B, L], F32R)
        silu_g = sb("silu_g", [P, B, L])
        z_a = sb("z_a", [P, L])
        z_log = sb("z_log", [P, L])
        gate = sb("gate", [P, B, L])
        u_tok = sb("u_tok", [P, TILES, DH, P])
        state = sb("state", [P, 2, L])
        o_acc = sb("o_acc", [P, L])
        o_stats = sb("o_stats", [P, TILES, 6])
        o_mv = sb("o_mv", [P, TILES, 2])
        o_var = sb("o_var", [P, TILES])
        o_rstd = sb("o_rstd", [P, TILES])
        o_hat = sb("o_hat", [P, TILES, HID])
        og = sb("og", [P, L])
        r_stats = sb("r_stats", [P, TILES, 6])
        r_mv = sb("r_mv", [P, TILES, 2])
        r_var = sb("r_var", [P, TILES])
        r_rstd = sb("r_rstd", [P, TILES])
        x2 = sb("x2", [P, TILES, HID])
        x2_hi = sb("x2_hi", [P, L], F32R)
        x2_lo = sb("x2_lo", [P, L], F32R)

        silu_a = sb("silu_a", [P, 2, L])
        yT = sb("yT", [P, L])
        e_stats = sb("e_stats", [P, TILES, 6])
        e_mv = sb("e_mv", [P, TILES, 2])
        e_var = sb("e_var", [P, TILES])
        e_rstd = sb("e_rstd", [P, TILES])

        A = [ctx.enter_context(nc.psum_tensor(f"att{i}", [P, L], F32)) for i in range(4)]
        F = [ctx.enter_context(nc.psum_tensor(f"ffn{i}", [P, L], F32)) for i in range(4)]

        x_loaded = [sem(f"x_loaded{b}") for b in range(B)]
        proj_loaded = sem("proj_loaded")
        gk_loaded = sem("gk_loaded")
        vecs_loaded = sem("vecs_loaded")
        vecs_turned = sem("vecs_turned")
        vecs_ready = sem("vecs_ready")
        wout_loaded = sem("wout_loaded")
        w12_loaded = sem("w12_loaded")
        h1_loaded = sem("h1_loaded")
        h2_loaded = sem("h2_loaded")
        w3_loaded = sem("w3_loaded")
        consts_zero = sem("consts_zero")
        consts_ready = sem("consts_ready")
        rep_ready = sem("rep_ready")
        proj_hi_ready = sem("proj_hi_ready")
        proj_lo_ready = sem("proj_lo_ready")
        gk1T_ready = sem("gk1T_ready")
        gk1T_copied = sem("gk1T_copied")
        gk12_ready = sem("gk12_ready")
        wT_ready = sem("wT_ready")
        wT_hi_ready = sem("wT_hi_ready")
        wT_lo_ready = sem("wT_lo_ready")
        xT_ready = sem("xT_ready")
        x_hi_ready = sem("x_hi_ready")
        x_lo_ready = sem("x_lo_ready")
        kv_ready = sem("kv_ready")
        kv_copied = sem("kv_copied")
        z_ready = sem("z_ready")
        q_ready = sem("q_ready")
        g_ready = sem("g_ready")
        q_hi_ready = sem("q_hi_ready")
        q_lo_ready = sem("q_lo_ready")
        silu_g_ready = sem("silu_g_ready")
        z_abs_ready = sem("z_abs_ready")
        z_min_ready = sem("z_min_ready")
        z_exp_ready = sem("z_exp_ready")
        z_ln_ready = sem("z_ln_ready")
        z_log_ready = sem("z_log_ready")
        gate_ready = sem("gate_ready")
        u_ready = sem("u_ready")
        uT_ready = sem("uT_ready")
        q_rep_ready = sem("q_rep_ready")
        scanned = sem("scanned")
        y_ready = sem("y_ready")
        summed = sem("summed")
        oT_ready = sem("oT_ready")
        o_stats_ready = sem("o_stats_ready")
        stats_seen = sem("stats_seen")
        o_mv_ready = sem("o_mv_ready")
        o_var_ready = sem("o_var_ready")
        o_rstd_ready = sem("o_rstd_ready")
        o_hat_ready = sem("o_hat_ready")
        o_hatT_ready = sem("o_hatT_ready")
        affine_done = sem("affine_done")
        gated = sem("gated")
        r_ready = sem("r_ready")
        x1_ready = sem("x1_ready")
        r_stats_ready = sem("r_stats_ready")
        r_mv_ready = sem("r_mv_ready")
        r_var_ready = sem("r_var_ready")
        r_rstd_ready = sem("r_rstd_ready")
        x2_ready = sem("x2_ready")
        x2T_ready = sem("x2T_ready")
        x2_kept = sem("x2_kept")
        x2_hi_ready = sem("x2_hi_ready")
        x2_lo_ready = sem("x2_lo_ready")
        ffn_banks_free = sem("ffn_banks_free")
        a_ready = sem("a_ready")
        b_ready = sem("b_ready")
        silu_a_ready = sem("silu_a_ready")
        f1_ready = sem("f1_ready")
        f1_hi_ready = sem("f1_hi_ready")
        f1_lo_ready = sem("f1_lo_ready")
        hid_ready = sem("hid_ready")
        gelu_hi_ready = sem("gelu_hi_ready")
        gelu_ready = sem("gelu_ready")
        gelu_lo_ready = sem("gelu_lo_ready")
        w3_ready = sem("w3_ready")
        yT_ready = sem("yT_ready")
        y_tok_ready = sem("y_tok_ready")
        e_sum_ready = sem("e_sum_ready")
        e_stats_ready = sem("e_stats_ready")
        e_mv_ready = sem("e_mv_ready")
        e_var_ready = sem("e_var_ready")
        e_rstd_ready = sem("e_rstd_ready")
        out_ready = sem("out_ready")
        out_stored = sem("out_stored")

        x_rows = x.rearrange("b (j p) c -> b p j c", p=P)
        out_rows = out.rearrange("b (j p) c -> b p j c", p=P)

        def tile(j):
            return slice(j * P, (j + 1) * P)

        weight_banks = []
        for layer in range(2):
            weight_banks.append(([w12_raw[:, layer, o, :] for o in range(OB)],
                                 w12_hi[:, layer, :], w12_lo[:, layer, :], (w12_loaded, 32)))
        for layer, loaded in ((0, h1_loaded), (1, h2_loaded)):
            for c in range(OB):
                weight_banks.append(([h_raw[:, layer, o, tile(c)] for o in range(OB)],
                                     h_hi[:, layer, c, :], h_lo[:, layer, c, :], (loaded, 16)))
        weight_banks.append(([w3_raw[:, tile(c)] for c in range(OB)],
                             w3_hi[:, :, :].rearrange("p c d -> p (c d)"),
                             w3_lo[:, :, :].rearrange("p c d -> p (c d)"), (w3_loaded, 16)))
        WB = len(weight_banks)

        block = ctx.enter_context(nc.Block())

        @block.sync
        def _(sp):
            sp.dma_start(x_tok[:, 0], x_rows[0]).then_inc(x_loaded[0], 16)
            for n, w in enumerate((Wk, Wv, Wq, Wg)):
                sp.dma_start(proj_raw[:, n, :], w).then_inc(proj_loaded, 16)
            sp.dma_start(wgk1[:], Wgk1).then_inc(gk_loaded, 16)
            sp.dma_start(wgk2[:], Wgk2).then_inc(gk_loaded, 16)
            for n, v in enumerate((w1_s, w2_s, h1_s, h2_s)):
                sp.dma_start(vec_rows[n * OB:(n + 1) * OB, :],
                             v.rearrange("(o p) -> o p", p=P)).then_inc(vecs_loaded, 16)
            for n, v in enumerate((w3_s, bgk2, gamma, beta)):
                sp.dma_start(vec_rows[4 * OB + n:4 * OB + n + 1, :],
                             v.rearrange("(o p) -> o p", p=P)).then_inc(vecs_loaded, 16)
            for b in range(1, B):
                sp.dma_start(x_tok[:, b], x_rows[b]).then_inc(x_loaded[b], 16)
            for n, w in enumerate((w1_w, w2_w)):
                sp.dma_start(w12_raw[:, n], w.rearrange("(o p) c -> p o c", p=P)).then_inc(w12_loaded, 16)
            sp.dma_start(wout[:], Wout).then_inc(wout_loaded, 16)
            sp.dma_start(h_raw[:, 0], h1_w.rearrange("(o p) c -> p o c", p=P)).then_inc(h1_loaded, 16)
            sp.dma_start(h_raw[:, 1], h2_w.rearrange("(o p) c -> p o c", p=P)).then_inc(h2_loaded, 16)
            sp.dma_start(w3_raw[:], w3_w).then_inc(w3_loaded, 16)

            def store_out(b):
                sp.wait_ge(out_ready, TILES * (b + 1))
                sp.dma_start(out_rows[b], out_tok[:, b]).then_inc(out_stored, 16)

            with sp.Fori(0, B) as b:
                store_out(b)
            sp.wait_ge(out_stored, 16 * B)

        @block.gpsimd
        def _(pool):
            nc.gpsimd.memset(ident[:], 0.0).then_inc(consts_zero, 1)
            nc.gpsimd.memset(rep_f[:], 0.0).then_inc(consts_zero, 1)
            pool.wait_ge(consts_zero, 1)
            nc.gpsimd.affine_select(out=ident[:], in_=ident[:], compare_op=ALU.not_equal, fill=1.0, base=0,
                                    pattern=[[-1, P]], channel_multiplier=1).then_inc(consts_ready, 1)
            pool.wait_ge(consts_zero, 2)
            rep_v = rep_f[:].rearrange("p k (h v) -> p k h v", v=DH)
            nc.gpsimd.affine_select(out=rep_v, in_=rep_v, compare_op=ALU.not_equal, fill=1.0, base=0,
                                    pattern=[[-1, DH], [-DH, HEADS], [0, DH]],
                                    channel_multiplier=1).then_inc(consts_ready, 1)
            nc.gpsimd.memset(half_neg[:], -0.5).then_inc(consts_ready, 1)
            nc.gpsimd.memset(eps[:], EPS).then_inc(consts_ready, 1)
            pool.wait_ge(consts_ready, 4)

            def outer_products(b, tiles):
                for j in tiles:
                    if j == 0:
                        if not (isinstance(b, int) and b == 0):
                            pool.wait_ge(uT_ready, DH * b)
                    pool.wait_ge(kv_copied, 2 * b + j // 2 + 1)
                    k_b = kv_tok[:, b, j, 0:HID].rearrange("p (h k) -> p k h", k=DH)
                    v_b = kv_tok[:, b, j, HID:2 * HID].rearrange("p (h v) -> p h v", v=DH)
                    nc.gpsimd.tensor_tensor(
                        u_tok[:, j].rearrange("p k (h v) -> p k h v", v=DH),
                        v_b.unsqueeze(1).to_broadcast([P, DH, HEADS, DH]),
                        k_b.unsqueeze(3).to_broadcast([P, DH, HEADS, DH]), ALU.mult).then_inc(u_ready, 1)

            def sum_over_k(b):
                for k in range(1, DH):
                    pool.wait_ge(y_ready, DH * b + k + 1)
                    if k == 1:
                        if not (isinstance(b, int) and b == 0):
                            pool.wait_ge(oT_ready, b)
                        first = y[:, 0]
                    else:
                        pool.wait_ge(summed, (DH - 1) * b + k - 1)
                        first = o_acc[:]
                    nc.gpsimd.tensor_tensor(o_acc[:], first, y[:, k % 4], ALU.add).then_inc(summed, 1)

            def rstd_of(b, mv_ready, mv, var, var_ready, rstd, rstd_ready):
                pool.wait_ge(mv_ready, TILES * (b + 1))
                nc.gpsimd.tensor_tensor(var[:], mv[:, :, 1], eps[:], ALU.add).then_inc(var_ready, 1)
                pool.wait_ge(var_ready, b + 1)
                nc.gpsimd.tensor_tensor(rstd[:], var[:], half_neg[:], ALU.pow).then_inc(rstd_ready, 1)

            def o_rstd_of(b):
                rstd_of(b, o_mv_ready, o_mv, o_var, o_var_ready, o_rstd, o_rstd_ready)

            def r_rstd_of(b):
                rstd_of(b, r_mv_ready, r_mv, r_var, r_var_ready, r_rstd, r_rstd_ready)

            def e_rstd_of(b):
                rstd_of(b, e_mv_ready, e_mv, e_var, e_var_ready, e_rstd, e_rstd_ready)

            def attention(b, follows):
                sum_over_k(b)
                o_rstd_of(b)
                if follows:
                    outer_products(b + 1, (0, 1))
                r_rstd_of(b)
                if follows:
                    outer_products(b + 1, (2, 3))

            outer_products(0, range(TILES))
            attention(0, True)
            with pool.Fori(0, B - 2) as i:
                attention(i + 1, True)
                e_rstd_of(i)
            attention(B - 1, False)
            e_rstd_of(B - 2)
            e_rstd_of(B - 1)

        @block.tensor
        def _(pe):
            def three_passes(ps, wh, wl, mh, ml, start=True, stop=True, before_lo=None):
                nc.tensor.matmul(ps, wh, mh, start=start, stop=False)
                nc.tensor.matmul(ps, wl, mh, start=False, stop=False)
                if before_lo is not None:
                    pe.wait_ge(*before_lo)
                return nc.tensor.matmul(ps, wh, ml, start=False, stop=stop)

            def front_banks(b):
                return A if b == 0 else F

            def transpose_x(b):
                pe.wait_ge(x_loaded[b], 16)
                if b >= 2:
                    pe.wait_ge(q_lo_ready, b)
                for j in range(TILES):
                    last = nc.tensor.transpose(front_banks(b)[0][:, tile(j)], x_tok[:, b, j, :], ident[:])
                last.then_inc(xT_ready, 1)

            def project_kv(b):
                pe.wait_ge(x_hi_ready, b + 1)
                pe.wait_ge(x_lo_ready, b + 1)
                kv_h = proj_hi[:, 0:2, :].rearrange("p n c -> p (n c)")
                kv_l = proj_lo[:, 0:2, :].rearrange("p n c -> p (n c)")
                for pair in range(2):
                    if b >= 2:
                        pe.wait_ge(kv_copied, 2 * (b - 1) + pair + 1)
                    for half in range(2):
                        t = tile(2 * pair + half)
                        ps = front_banks(b)[1 + pair][:, half * 2 * HID:(half + 1) * 2 * HID]
                        nc.tensor.matmul(ps, x_hi[:, b, t], kv_h, start=True, stop=False)
                        nc.tensor.matmul(ps, x_hi[:, b, t], kv_l, start=False, stop=False)
                        last = nc.tensor.matmul(ps, x_lo[:, b, t], kv_h, start=False, stop=True)
                    last.then_inc(kv_ready, 1)

            def project(b, n, bank, ready):
                three_passes(bank[:], proj_hi[:, n], proj_lo[:, n], x_hi[:, b], x_lo[:, b]).then_inc(ready, 1)

            def project_z(b):
                if b == 0:
                    pe.wait_ge(proj_lo_ready, 2)
                if b >= 2:
                    pe.wait_ge(z_log_ready, b)
                project(b, 4, front_banks(b)[3], z_ready)

            def project_q(b):
                project(b, 2, front_banks(b)[0], q_ready)

            def project_g(b):
                pe.wait_ge(*((q_lo_ready, B), (kv_copied, 2 * B - 1), (kv_copied, 2 * B), (z_log_ready, B))[b])
                project(b, 3, F[b], g_ready)

            def replicate_q(b, k):
                if k == 0:
                    if isinstance(b, int) and b == 0:
                        pe.wait_ge(q_lo_ready, 1)
                    else:
                        pe.wait_ge(x2_ready, TILES * b)
                elif k == 1:
                    if isinstance(b, int) and b == 0:
                        pe.wait_ge(kv_copied, 1)
                    else:
                        pe.wait_ge(x2_lo_ready, b)
                else:
                    pe.wait_ge(y_ready, DH * b + k - 1)
                nc.tensor.matmul(A[k % 2][:], rep[:, k], q_hi[:, b], start=True, stop=False)
                nc.tensor.matmul(A[k % 2][:], rep[:, k], q_lo[:, b], start=False, stop=True).then_inc(q_rep_ready, 1)

            def transpose_u(b, k):
                if k == 0:
                    pe.wait_ge(u_ready, TILES * (b + 1))
                    if not (isinstance(b, int) and b == 0):
                        pe.wait_ge(o_hat_ready, TILES * b)
                elif k == 1:
                    if isinstance(b, int) and b == 0:
                        pe.wait_ge(z_log_ready, 1)
                    else:
                        pe.wait_ge(gated, b)
                else:
                    pe.wait_ge(scanned, DH * b + k - 1)
                for j in range(TILES):
                    last = nc.tensor.transpose(A[2 + k % 2][:, tile(j)], u_tok[:, j, k], ident[:])
                last.then_inc(uT_ready, 1)

            def transpose_o(b):
                pe.wait_ge(summed, (DH - 1) * (b + 1))
                for j in range(TILES):
                    last = nc.tensor.transpose(A[2][:, tile(j)], o_acc[:, tile(j)], ident[:])
                last.then_inc(oT_ready, 1)

            def transpose_o_hat(b):
                for j in range(TILES):
                    pe.wait_ge(o_hat_ready, TILES * b + j + 1)
                    last = nc.tensor.transpose(A[3][:, tile(j)], o_hat[:, j], ident[:])
                last.then_inc(o_hatT_ready, 1)

            def project_out(b):
                pe.wait_ge(gated, b + 1)
                for j in range(TILES):
                    last = nc.tensor.matmul(A[0][:, tile(j)], og[:, tile(j)], wout[:], start=True, stop=True)
                last.then_inc(r_ready, 1)

            def transpose_x2(b):
                for j in range(TILES):
                    pe.wait_ge(x2_ready, TILES * b + j + 1)
                    last = nc.tensor.transpose(A[1][:, tile(j)], x2[:, j], ident[:])
                last.then_inc(x2T_ready, 1)

            def ffn_in(b, o):
                if o == 0:
                    pe.wait_ge(x2_hi_ready, b + 1)
                    pe.wait_ge(x2_lo_ready, b + 1)
                    pe.wait_ge(ffn_banks_free, b + 1)
                if o >= 2:
                    pe.wait_ge(silu_a_ready, OB * b + o - 1)
                fa, fb = F[(2 * o) % 4], F[(2 * o + 1) % 4]
                three_passes(fa[:], w12_hi[:, 0, tile(o)], w12_lo[:, 0, tile(o)],
                             x2_hi[:], x2_lo[:]).then_inc(a_ready, 1)
                if o >= 2:
                    pe.wait_ge(f1_lo_ready, OB * b + o - 1)
                three_passes(fb[:], w12_hi[:, 1, tile(o)], w12_lo[:, 1, tile(o)],
                             x2_hi[:], x2_lo[:]).then_inc(b_ready, 1)

            def ffn_hidden(b, layer, o):
                src_hi, src_lo = ((f1_hi, f1_lo), (f2_hi, f2_lo))[layer]
                if layer == 0:
                    if o in (0, 2):
                        pe.wait_ge(silu_a_ready, OB * b + OB - 1 + o // 2)
                    else:
                        pe.wait_ge(f1_lo_ready, OB * b + OB - 1 + o // 2)
                else:
                    pe.wait_ge(gelu_lo_ready, 2 * OB * b + o + 1)
                for c in range(OB):
                    if layer == 0:
                        pe.wait_ge(f1_hi_ready, OB * b + c + 1)
                    else:
                        pe.wait_ge(gelu_hi_ready, 2 * OB * b + c + 1)
                    nc.tensor.matmul(F[o][:], h_hi[:, layer, c, tile(o)], src_hi[:, c], start=(c == 0), stop=False)
                    nc.tensor.matmul(F[o][:], h_lo[:, layer, c, tile(o)], src_hi[:, c], start=False, stop=False)
                for c in range(OB):
                    if layer == 0:
                        pe.wait_ge(f1_lo_ready, OB * b + c + 1)
                    else:
                        pe.wait_ge(gelu_lo_ready, 2 * OB * b + c + 1)
                    last = nc.tensor.matmul(F[o][:], h_hi[:, layer, c, tile(o)], src_lo[:, c],
                                            start=False, stop=(c == OB - 1))
                last.then_inc(hid_ready, 1)

            def ffn_out(b):
                for c in range(OB):
                    pe.wait_ge(gelu_hi_ready, 2 * OB * b + OB + c + 1)
                    if c == 0:
                        pe.wait_ge(gelu_lo_ready, 2 * OB * b + OB + 1)
                    nc.tensor.matmul(F[0][:], w3_hi[:, c], f1_hi[:, c], start=(c == 0), stop=False)
                    nc.tensor.matmul(F[0][:], w3_lo[:, c], f1_hi[:, c], start=False, stop=False)
                for c in range(OB):
                    pe.wait_ge(gelu_lo_ready, 2 * OB * b + OB + c + 1)
                    last = nc.tensor.matmul(F[0][:], w3_hi[:, c], f1_lo[:, c], start=False, stop=(c == OB - 1))
                last.then_inc(w3_ready, 1)

            def transpose_y(b):
                pe.wait_ge(yT_ready, b + 1)
                for j in range(TILES):
                    last = nc.tensor.transpose(F[1][:, tile(j)], yT[:, tile(j)], ident[:])
                last.then_inc(y_tok_ready, 1)

            def weight_bank(n):
                blocks, _, _, loaded = weight_banks[n]
                pe.wait_ge(*loaded)
                if n < 4:
                    pe.wait_ge(silu_g_ready, n + 1)
                else:
                    pe.wait_ge(wT_lo_ready, n - 3)
                for j, w in enumerate(blocks):
                    last = nc.tensor.transpose(F[n % 4][:, tile(j)], w, ident[:])
                last.then_inc(wT_ready, 1)

            def step(a, f):
                replicate_q(a, 0)
                replicate_q(a, 1)
                transpose_u(a, 0)
                transpose_u(a, 1)
                for o in range(OB):
                    ffn_in(f, o)
                    transpose_u(a, 2 + o)
                    replicate_q(a, 2 + o)
                ffn_hidden(f, 0, 0)
                transpose_u(a, 6)
                replicate_q(a, 6)
                ffn_hidden(f, 0, 1)
                transpose_u(a, 7)
                replicate_q(a, 7)
                ffn_hidden(f, 0, 2)
                ffn_hidden(f, 0, 3)
                transpose_o(a)
                ffn_hidden(f, 1, 0)
                ffn_hidden(f, 1, 1)
                transpose_o_hat(a)
                ffn_hidden(f, 1, 2)
                project_out(a)
                ffn_hidden(f, 1, 3)
                ffn_out(f)
                transpose_x2(a)
                transpose_y(f)

            pe.wait_ge(consts_ready, 1)
            transpose_x(0)
            pe.wait_ge(gk_loaded, 32)
            nc.tensor.transpose(A[3][0:RANK, 0:P], wgk1[:], ident[:]).then_inc(gk1T_ready, 1)
            pe.wait_ge(vecs_loaded, 16 * 8)
            nc.tensor.transpose(A[1][:, 0:VECS], vec_rows[:], ident[0:VECS, 0:VECS]).then_inc(vecs_turned, 1)
            pe.wait_ge(gk1T_copied, 1)
            nc.tensor.matmul(A[3][:, P:2 * P], wgk1T[:], wgk2[:], start=True, stop=True).then_inc(gk12_ready, 1)
            pe.wait_ge(vecs_ready, 1)
            pe.wait_ge(proj_lo_ready, 1)
            project_kv(0)
            project_q(0)
            project_z(0)
            transpose_x(1)
            pe.wait_ge(rep_ready, 1)
            replicate_q(0, 0)
            replicate_q(0, 1)
            project_kv(1)
            project_z(1)
            project_q(1)
            transpose_u(0, 0)
            transpose_u(0, 1)
            transpose_x(2)
            project_kv(2)
            project_z(2)
            project_q(2)
            for k in (2, 3):
                transpose_u(0, k)
                replicate_q(0, k)
            transpose_x(3)
            project_kv(3)
            project_z(3)
            project_q(3)
            for k in (4, 5, 6):
                transpose_u(0, k)
                replicate_q(0, k)
            for b in range(B):
                project_g(b)
            transpose_u(0, 7)
            replicate_q(0, 7)
            weight_bank(0)
            weight_bank(1)
            transpose_o(0)
            weight_bank(2)
            weight_bank(3)
            weight_bank(4)
            transpose_o_hat(0)
            pe.wait_ge(wout_loaded, 16)
            project_out(0)
            weight_bank(5)
            weight_bank(6)
            weight_bank(7)
            transpose_x2(0)
            weight_bank(8)
            weight_bank(9)
            weight_bank(10)

            with pe.Fori(0, B - 2) as i:
                step(i + 1, i)
            step(B - 1, B - 2)

            last_row = B - 1
            for o in range(OB):
                ffn_in(last_row, o)
            for layer in range(2):
                for o in range(OB):
                    ffn_hidden(last_row, layer, o)
            ffn_out(last_row)
            transpose_y(last_row)

        @block.scalar
        def _(act):
            def front_banks(b):
                return A if b == 0 else F

            def round_x(b):
                act.wait_ge(xT_ready, b + 1)
                nc.scalar.copy(x_hi[:, b], front_banks(b)[0][:]).then_inc(x_hi_ready, 1)

            def copy_kv(b):
                for pair in range(2):
                    act.wait_ge(kv_ready, 2 * b + pair + 1)
                    nc.scalar.copy(kv_tok[:, b, 2 * pair:2 * pair + 2, :].rearrange("p j c -> p (j c)"),
                                   front_banks(b)[1 + pair][:]).then_inc(kv_copied, 1)

            def round_q(b):
                act.wait_ge(q_ready, b + 1)
                nc.scalar.copy(q_hi[:, b], front_banks(b)[0][:]).then_inc(q_hi_ready, 1)

            def log_part(b):
                act.wait_ge(z_ready, b + 1)
                if b >= 1:
                    act.wait_ge(z_log_ready, b)
                nc.scalar.activation(z_a[:], front_banks(b)[3][:], ACT.Abs, bias=bgk2_col).then_inc(z_abs_ready, 1)
                act.wait_ge(z_abs_ready, b + 1)
                nc.scalar.activation(z_a[:], z_a[:], ACT.Exp, scale=-1.0).then_inc(z_exp_ready, 1)
                act.wait_ge(z_exp_ready, b + 1)
                nc.scalar.activation(z_a[:], z_a[:], ACT.Ln, bias=1.0).then_inc(z_ln_ready, 1)

            def gates(b):
                act.wait_ge(z_log_ready, b + 1)
                nc.scalar.activation(gate[:, b], z_log[:], ACT.Exp, scale=GATE_SCALE).then_inc(gate_ready, 1)

            def silu_of_g(b):
                act.wait_ge(g_ready, b + 1)
                nc.scalar.activation(silu_g[:, b], F[b][:], ACT.Silu).then_inc(silu_g_ready, 1)

            def affine(b):
                act.wait_ge(o_hatT_ready, b + 1)
                nc.scalar.activation(A[3][:], A[3][:], ACT.Identity, scale=gamma_col,
                                     bias=beta_col).then_inc(affine_done, 1)

            def keep_x2(b):
                act.wait_ge(x2_ready, TILES * (b + 1))
                nc.scalar.copy(x_tok[:, b], x2[:]).then_inc(x2_kept, 1)

            def round_x2(b):
                act.wait_ge(x2T_ready, b + 1)
                if not (isinstance(b, int) and b == 0):
                    act.wait_ge(b_ready, OB * b)
                nc.scalar.copy(x2_hi[:], A[1][:]).then_inc(x2_hi_ready, 1)

            def ffn_silu(b, o):
                act.wait_ge(a_ready, OB * b + o + 1)
                if o >= 2:
                    act.wait_ge(f1_ready, OB * b + o - 1)
                nc.scalar.activation(silu_a[:, o % 2], F[(2 * o) % 4][:], ACT.Silu,
                                     scale=scales[:, 0, o:o + 1]).then_inc(silu_a_ready, 1)

            def ffn_round(b, o):
                act.wait_ge(f1_ready, OB * b + o + 1)
                nc.scalar.copy(f1_hi[:, o], F[(2 * o + 1) % 4][:]).then_inc(f1_hi_ready, 1)

            def ffn_gelu(b, layer, o):
                dst = (f2_hi, f1_hi)[layer]
                n = 2 * OB * b + OB * layer + o + 1
                if layer == 1 and o == 0:
                    act.wait_ge(hid_ready, 2 * OB * b + OB)
                act.wait_ge(hid_ready, n)
                nc.scalar.activation(dst[:, o], F[o][:], ACT.Gelu,
                                     scale=scales[:, 2 + layer, o:o + 1]).then_inc(gelu_hi_ready, 1)
                act.wait_ge(gelu_hi_ready, n)
                nc.scalar.activation(F[o][:], F[o][:], ACT.Gelu,
                                     scale=scales[:, 2 + layer, o:o + 1]).then_inc(gelu_ready, 1)

            def scale_y(b):
                act.wait_ge(w3_ready, b + 1)
                nc.scalar.activation(yT[:], F[0][:], ACT.Identity, scale=w3_col).then_inc(yT_ready, 1)

            def weight_bank_hi(n):
                act.wait_ge(wT_ready, n + 1)
                nc.scalar.copy(weight_banks[n][1], F[n % 4][:]).then_inc(wT_hi_ready, 1)

            def step(a, f):
                for o in range(OB):
                    ffn_silu(f, o)
                    if o >= 1:
                        ffn_round(f, o - 1)
                ffn_round(f, OB - 1)
                for o in range(OB):
                    ffn_gelu(f, 0, o)
                ffn_gelu(f, 1, 0)
                ffn_gelu(f, 1, 1)
                affine(a)
                ffn_gelu(f, 1, 2)
                ffn_gelu(f, 1, 3)
                scale_y(f)
                keep_x2(a)
                round_x2(a)

            nc.scalar.preload_act_table_set("natural_log_exp_and_others")
            round_x(0)
            act.wait_ge(proj_loaded, 64)
            nc.scalar.copy(proj_hi[:, 0:4], proj_raw[:]).then_inc(proj_hi_ready, 1)
            act.wait_ge(gk1T_ready, 1)
            nc.scalar.copy(wgk1T[:], A[3][0:RANK, 0:P]).then_inc(gk1T_copied, 1)
            act.wait_ge(vecs_turned, 1)
            nc.scalar.copy(vec_cols[:], A[1][:, 0:VECS]).then_inc(vecs_ready, 1)
            act.wait_ge(gk12_ready, 1)
            nc.scalar.copy(proj_hi[:, 4], A[3][:, P:2 * P]).then_inc(proj_hi_ready, 1)
            copy_kv(0)
            round_q(0)
            act.wait_ge(vecs_ready, 1)
            log_part(0)
            round_x(1)
            act.wait_ge(consts_ready, 2)
            nc.scalar.copy(rep[:], rep_f[:]).then_inc(rep_ready, 1)
            gates(0)
            for b in range(1, B):
                copy_kv(b)
                log_part(b)
                round_q(b)
                gates(b)
                if b + 1 < B:
                    round_x(b + 1)
            for b in range(B):
                silu_of_g(b)
            weight_bank_hi(0)
            weight_bank_hi(1)
            weight_bank_hi(2)
            weight_bank_hi(3)
            weight_bank_hi(4)
            affine(0)
            weight_bank_hi(5)
            weight_bank_hi(6)
            weight_bank_hi(7)
            keep_x2(0)
            round_x2(0)
            weight_bank_hi(8)
            weight_bank_hi(9)
            weight_bank_hi(10)

            with act.Fori(0, B - 2) as i:
                step(i + 1, i)
            step(B - 1, B - 2)

            last_row = B - 1
            for o in range(OB):
                ffn_silu(last_row, o)
                if o >= 1:
                    ffn_round(last_row, o - 1)
            ffn_round(last_row, OB - 1)
            for layer in range(2):
                for o in range(OB):
                    ffn_gelu(last_row, layer, o)
            scale_y(last_row)

        @block.vector
        def _(dve):
            def front_banks(b):
                return A if b == 0 else F

            def rest_of_x(b):
                dve.wait_ge(x_hi_ready, b + 1)
                nc.vector.tensor_tensor(x_lo[:, b], front_banks(b)[0][:], x_hi[:, b].bitcast(F32),
                                        ALU.subtract).then_inc(x_lo_ready, 1)

            def min_z(b):
                bank = front_banks(b)[3]
                dve.wait_ge(z_abs_ready, b + 1)
                nc.vector.tensor_scalar(bank[:], bank[:], bgk2_col, 0.0, ALU.add, ALU.min).then_inc(z_min_ready, 1)

            def log_gate(b):
                dve.wait_ge(z_min_ready, b + 1)
                dve.wait_ge(z_ln_ready, b + 1)
                if b >= 1:
                    dve.wait_ge(gate_ready, b)
                nc.vector.tensor_tensor(z_log[:], front_banks(b)[3][:], z_a[:], ALU.subtract).then_inc(z_log_ready, 1)

            def rest_of_q(b):
                dve.wait_ge(q_hi_ready, b + 1)
                nc.vector.tensor_tensor(q_lo[:, b], front_banks(b)[0][:], q_hi[:, b].bitcast(F32),
                                        ALU.subtract).then_inc(q_lo_ready, 1)

            def scan(b, k):
                dve.wait_ge(uT_ready, DH * b + k + 1)
                if k == 0:
                    dve.wait_ge(gate_ready, b + 1)
                if k >= 2:
                    dve.wait_ge(y_ready, DH * b + k - 1)
                elif not (isinstance(b, int) and b == 0):
                    dve.wait_ge(y_ready, DH * b)
                nc.vector.tensor_tensor_scan(state[:, k % 2], gate[:, b], A[2 + k % 2][:], 0.0,
                                             ALU.mult, ALU.add).then_inc(scanned, 1)

            def read_out(b, k):
                dve.wait_ge(q_rep_ready, DH * b + k + 1)
                dve.wait_ge(scanned, DH * b + k + 1)
                if k >= 4:
                    dve.wait_ge(summed, (DH - 1) * b + max(k - 4, 1))
                elif not (isinstance(b, int) and b == 0):
                    dve.wait_ge(summed, (DH - 1) * b)
                nc.vector.tensor_tensor(y[:, k % 4], A[k % 2][:], state[:, k % 2], ALU.mult).then_inc(y_ready, 1)

            def statistics(b, bank, stats, stats_ready, mv, mv_ready):
                for j in range(TILES):
                    nc.vector.bn_stats(stats[:, j], bank[:, tile(j)]).then_inc(stats_ready, 1)
                for j in range(TILES):
                    if j == 0:
                        dve.wait_ge(stats_ready, TILES * (b + 1))
                        dve.sem_inc(stats_seen, 1)
                    nc.vector.bn_aggr(mv[:, j], stats[:, j]).then_inc(mv_ready, 1)

            def normalise(dst, dst_ready, bank, mv, rstd):
                for j in range(TILES):
                    nc.vector.tensor_scalar(dst[:, j], bank[:, tile(j)], mv[:, j, 0:1], rstd[:, j:j + 1],
                                            ALU.subtract, ALU.mult).then_inc(dst_ready, 1)

            def o_statistics(b):
                dve.wait_ge(oT_ready, b + 1)
                statistics(b, A[2], o_stats, o_stats_ready, o_mv, o_mv_ready)

            def o_normalise(b):
                dve.wait_ge(o_rstd_ready, b + 1)
                normalise(o_hat, o_hat_ready, A[2], o_mv, o_rstd)

            def apply_gate(b):
                dve.wait_ge(affine_done, b + 1)
                if not (isinstance(b, int) and b == 0):
                    dve.wait_ge(r_ready, b)
                nc.vector.tensor_tensor(og[:], A[3][:], silu_g[:, b], ALU.mult).then_inc(gated, 1)

            def add_x(b):
                dve.wait_ge(r_ready, b + 1)
                nc.vector.tensor_tensor(A[0][:], A[0][:], x_tok[:, b].rearrange("p j c -> p (j c)"),
                                        ALU.add).then_inc(x1_ready, 1)
                dve.wait_ge(x1_ready, b + 1)
                statistics(b, A[0], r_stats, r_stats_ready, r_mv, r_mv_ready)

            def x2_normalise(b):
                dve.wait_ge(r_rstd_ready, b + 1)
                if not (isinstance(b, int) and b == 0):
                    dve.wait_ge(x2T_ready, b)
                    dve.wait_ge(x2_kept, b)
                normalise(x2, x2_ready, A[0], r_mv, r_rstd)

            def rest_of_x2(b):
                dve.wait_ge(x2_hi_ready, b + 1)
                nc.vector.tensor_tensor(x2_lo[:], A[1][:], x2_hi[:].bitcast(F32), ALU.subtract).then_inc(x2_lo_ready, 1)

            def ffn_product(b, o):
                bank = F[(2 * o + 1) % 4]
                dve.wait_ge(b_ready, OB * b + o + 1)
                dve.wait_ge(silu_a_ready, OB * b + o + 1)
                nc.vector.scalar_tensor_tensor(bank[:], bank[:], scales[:, 1, o:o + 1], silu_a[:, o % 2],
                                               ALU.mult, ALU.mult).then_inc(f1_ready, 1)

            def ffn_rest(b, o):
                dve.wait_ge(f1_hi_ready, OB * b + o + 1)
                nc.vector.tensor_tensor(f1_lo[:, o], F[(2 * o + 1) % 4][:], f1_hi[:, o].bitcast(F32),
                                        ALU.subtract).then_inc(f1_lo_ready, 1)

            def gelu_rest(b, layer, o):
                hi, lo = ((f2_hi, f2_lo), (f1_hi, f1_lo))[layer]
                dve.wait_ge(gelu_ready, 2 * OB * b + OB * layer + o + 1)
                nc.vector.tensor_tensor(lo[:, o], F[o][:], hi[:, o].bitcast(F32),
                                        ALU.subtract).then_inc(gelu_lo_ready, 1)

            def add_x2(b):
                dve.wait_ge(y_tok_ready, b + 1)
                dve.wait_ge(x2_kept, b + 1)
                nc.vector.tensor_tensor(F[1][:], F[1][:], x_tok[:, b].rearrange("p j c -> p (j c)"), ALU.add).then_inc(e_sum_ready, 1)
                dve.wait_ge(e_sum_ready, b + 1)
                statistics(b, F[1], e_stats, e_stats_ready, e_mv, e_mv_ready)

            def out_normalise(b):
                dve.wait_ge(e_rstd_ready, b + 1)
                normalise(out_tok[:, b], out_ready, F[1], e_mv, e_rstd)
                dve.wait_ge(out_ready, TILES * (b + 1))
                dve.sem_inc(ffn_banks_free, 1)

            def weight_bank_lo(n):
                dve.wait_ge(wT_hi_ready, n + 1)
                _, hi, lo, _ = weight_banks[n]
                nc.vector.tensor_tensor(lo, F[n % 4][:], hi.bitcast(F32), ALU.subtract).then_inc(wT_lo_ready, 1)

            def step(a, f):
                scan(a, 0)
                scan(a, 1)
                read_out(a, 0)
                for o in range(OB):
                    ffn_product(f, o)
                    scan(a, 2 + o)
                    read_out(a, 1 + o)
                    ffn_rest(f, o)
                scan(a, 6)
                read_out(a, 5)
                gelu_rest(f, 0, 0)
                scan(a, 7)
                read_out(a, 6)
                read_out(a, 7)
                gelu_rest(f, 0, 1)
                gelu_rest(f, 0, 2)
                gelu_rest(f, 0, 3)
                o_statistics(a)
                gelu_rest(f, 1, 0)
                o_normalise(a)
                gelu_rest(f, 1, 1)
                apply_gate(a)
                gelu_rest(f, 1, 2)
                add_x(a)
                gelu_rest(f, 1, 3)
                x2_normalise(a)
                rest_of_x2(a)
                add_x2(f)
                out_normalise(f)

            rest_of_x(0)
            dve.wait_ge(proj_hi_ready, 1)
            nc.vector.tensor_tensor(proj_lo[:, 0:4], proj_raw[:], proj_hi[:, 0:4].bitcast(F32),
                                    ALU.subtract).then_inc(proj_lo_ready, 1)
            dve.wait_ge(proj_hi_ready, 2)
            nc.vector.tensor_tensor(proj_lo[:, 4], A[3][:, P:2 * P], proj_hi[:, 4].bitcast(F32),
                                    ALU.subtract).then_inc(proj_lo_ready, 1)
            rest_of_q(0)
            dve.wait_ge(vecs_ready, 1)
            min_z(0)
            rest_of_x(1)
            log_gate(0)
            min_z(1)
            rest_of_q(1)
            log_gate(1)
            scan(0, 0)
            rest_of_x(2)
            scan(0, 1)
            read_out(0, 0)
            min_z(2)
            rest_of_q(2)
            scan(0, 2)
            read_out(0, 1)
            log_gate(2)
            rest_of_x(3)
            scan(0, 3)
            read_out(0, 2)
            min_z(3)
            rest_of_q(3)
            scan(0, 4)
            read_out(0, 3)
            log_gate(3)
            scan(0, 5)
            read_out(0, 4)
            scan(0, 6)
            read_out(0, 5)
            scan(0, 7)
            read_out(0, 6)
            read_out(0, 7)
            weight_bank_lo(0)
            weight_bank_lo(1)
            o_statistics(0)
            weight_bank_lo(2)
            weight_bank_lo(3)
            o_normalise(0)
            weight_bank_lo(4)
            apply_gate(0)
            add_x(0)
            weight_bank_lo(5)
            weight_bank_lo(6)
            x2_normalise(0)
            weight_bank_lo(7)
            rest_of_x2(0)
            weight_bank_lo(8)
            weight_bank_lo(9)
            weight_bank_lo(10)
            dve.wait_ge(wT_lo_ready, WB)
            dve.sem_inc(ffn_banks_free, 1)

            with dve.Fori(0, B - 2) as i:
                step(i + 1, i)
            step(B - 1, B - 2)

            last_row = B - 1
            for o in range(OB):
                ffn_product(last_row, o)
                ffn_rest(last_row, o)
            for layer in range(2):
                for o in range(OB):
                    gelu_rest(last_row, layer, o)
            add_x2(last_row)
            out_normalise(last_row)


_INS = ['L0_attn_x', 'L0_attn_Wq', 'L0_attn_Wk', 'L0_attn_Wv', 'L0_attn_Wg', 'L0_attn_Wgk1', 'L0_attn_Wgk2',
        'L0_attn_bgk2', 'L0_attn_gamma', 'L0_attn_beta', 'L0_attn_Wout', 'L0_ffn_w1_w', 'L0_ffn_w1_s',
        'L0_ffn_w2_w', 'L0_ffn_w2_s', 'L0_ffn_h1_w', 'L0_ffn_h1_s', 'L0_ffn_h2_w', 'L0_ffn_h2_s',
        'L0_ffn_w3_w', 'L0_ffn_w3_s']


def kernel(**inputs):
    import numpy as np
    import concourse.bacc as bacc
    from concourse.bass_utils import run_bass_kernel_spmd

    nc = bacc.Bacc("TRN2", target_bir_lowering=False, num_devices=1)
    arrays, args = {}, []
    for name in _INS:
        a = np.ascontiguousarray(inputs[name])
        arrays[f"in_{name}"] = a
        args.append(nc.dram_tensor(f"in_{name}", a.shape, mybir.dt.from_np(a.dtype), kind="ExternalInput").ap())
    out = nc.dram_tensor("out_0", inputs['L0_attn_x'].shape, F32, kind="ExternalOutput").ap()
    gla_ffn_kernel(nc, *args, out)
    r = run_bass_kernel_spmd(nc, [arrays], core_ids=[0])
    return r.results[0]["out_0"]
```

```python
from contextlib import ExitStack

import concourse.bass as bass
from concourse import mybir

P = 128
F32 = mybir.dt.float32
F32R = mybir.dt.float32r
ALU = mybir.AluOpType
ACT = mybir.ActivationFunctionType
EPS = 1e-5
GATE_SCALE = 1.0 / 16.0
SILU_SET, GELU_SET = "silu_and_others", "gelu_and_others"


def gla_ffn_kernel(nc, x, Wq, Wk, Wv, Wg, Wgk1, Wgk2, bgk2, gamma, beta, Wout,
                   w1_w, w1_s, w2_w, w2_s, h1_w, h1_s, h2_w, h2_s, w3_w, w3_s, out):
    B, L, HID = x.shape
    RANK = Wgk1.shape[1]
    D_HID = w1_w.shape[0]
    HEADS = 16
    DH = HID // HEADS
    TILES = L // P
    OB = D_HID // P
    assert HID == P and L == 512 and DH == 8 and OB == 4

    with ExitStack() as ctx:
        def sb(name, shape, dt=F32):
            return ctx.enter_context(nc.sbuf_tensor(name, shape, dt))

        def sem(name):
            return ctx.enter_context(nc.semaphore(name))

        def arena(name, nbytes, *tensors):
            base = -(-nc.sbuf_base // 32) * 32
            slab = sb(name, [P, nbytes // 4])
            return [nc.alloc_sbuf_tensor_at(n, shape, dt, offset=base + off) for n, shape, dt, off in tensors]

        ROW = L * 4
        x_hi, x_lo, f1_hi, f1_lo, lo_abs = arena(
            "place_f1", 2 * B * ROW, ("x_hi", [P, B, L], F32R, 0), ("x_lo", [P, B, L], F32R, B * ROW),
            ("f1_hi", [P, OB, L], F32R, 0), ("f1_lo", [P, OB, L], F32R, OB * ROW),
            ("lo_abs", [P, 2 * D_HID], F32, 2 * ROW))
        h_raw, f2_hi, f2_lo = arena(
            "place_f2", 2 * OB * ROW, ("h_raw", [P, 2, OB, D_HID], F32, 0),
            ("f2_hi", [P, OB, L], F32R, 0), ("f2_lo", [P, OB, L], F32R, OB * ROW))
        w12_raw, w3_raw, out_tok = arena(
            "place_out", B * ROW, ("w12_raw", [P, 2, OB, HID], F32, 0), ("w3_raw", [P, D_HID], F32, 2 * ROW),
            ("out_tok", [P, B, TILES, HID], F32, 0))
        rep_f, ones_f, y = arena(
            "place_y", 4 * ROW, ("rep_f", [P, DH, P], F32, 0), ("ones_f", [1, L], F32, 3 * ROW), ("y", [P, 4, L], F32, 0))

        x_tok = sb("x_tok", [P, B, TILES, HID])
        proj_raw = sb("proj_raw", [P, 4, HID])
        proj_hi = sb("proj_hi", [P, 5, HID], F32R)
        proj_lo = sb("proj_lo", [P, 5, HID], F32R)
        wgk1 = sb("wgk1", [P, RANK])
        wgk1T = sb("wgk1T", [RANK, HID])
        bias_row = sb("bias_row", [1, HID])
        bias_hi = sb("bias_hi", [1, HID], F32R)
        bias_lo = sb("bias_lo", [1, HID], F32R)
        wgk2 = sb("wgk2", [RANK, HID])
        wout = sb("wout", [P, HID])
        wout_beta = sb("wout_beta", [P, HID])
        VECS = 4 * OB + 3
        vec_rows = sb("vec_rows", [VECS, P])
        vec_cols = sb("vec_cols", [P, VECS])
        scales = vec_cols[:, 0:4 * OB].rearrange("p (n o) -> p n o", o=OB)
        w3_col, gamma_col, beta_col = (vec_cols[:, 4 * OB + n:4 * OB + n + 1] for n in range(3))
        w12_hi = sb("w12_hi", [P, 2, D_HID], F32R)
        w12_lo = sb("w12_lo", [P, 2, D_HID], F32R)
        h_hi = sb("h_hi", [P, 2, OB, D_HID], F32R)
        h_lo = sb("h_lo", [P, 2, OB, D_HID], F32R)
        w3_hi = sb("w3_hi", [P, OB, HID], F32R)
        w3_lo = sb("w3_lo", [P, OB, HID], F32R)
        ident = sb("ident", [P, P])
        center = sb("center", [P, P])
        rep = sb("rep", [P, DH, P], F32R)
        lo_sums = sb("lo_sums", [P, 6])
        lo_any = sb("lo_any", [P, 6])
        lo_flag = sb("lo_flag", [1, 1], mybir.dt.int32)
        ones = sb("ones", [P, 1])
        half_neg = sb("half_neg", [P, TILES])
        eps = sb("eps", [P, TILES])

        kv_tok = sb("kv_tok", [P, B, TILES, 2 * HID])
        q_hi = sb("q_hi", [P, B, L], F32R)
        q_lo = sb("q_lo", [P, B, L], F32R)
        silu_g = sb("silu_g", [P, B, L])
        z_a, x2_hi, x2_lo = arena(
            "place_x2", 2 * ROW, ("z_a", [P, 2, L], F32, 0), ("x2_hi", [P, L], F32R, 0), ("x2_lo", [P, L], F32R, ROW))
        gate = sb("gate", [P, B, L])
        u_tok = sb("u_tok", [P, TILES, DH, P])
        state = sb("state", [P, 3, L])
        o_acc = sb("o_acc", [P, L])
        o_stats = sb("o_stats", [P, TILES, 6])
        o_mv = sb("o_mv", [P, TILES, 2])
        o_var = sb("o_var", [P, TILES])
        o_rstd = sb("o_rstd", [P, TILES])
        og = sb("og", [P, L])
        r_stats = sb("r_stats", [P, TILES, 6])
        r_mv = sb("r_mv", [P, TILES, 2])
        r_var = sb("r_var", [P, TILES])
        r_rstd = sb("r_rstd", [P, TILES])
        x2 = sb("x2", [P, TILES, HID])

        SLOTS = 3
        full = sb("full", [P, SLOTS, L])
        e_minus = sb("e_minus", [P, TILES])
        e_shift = sb("e_shift", [P, TILES])
        ones_row, yT = arena("place_yT", ROW, ("ones_row", [1, L], F32R, 0), ("yT", [P, L], F32, 0))
        e_stats = sb("e_stats", [P, TILES, 6])
        e_mv = sb("e_mv", [P, TILES, 2])
        e_var = sb("e_var", [P, TILES])
        e_rstd = sb("e_rstd", [P, TILES])

        A = [ctx.enter_context(nc.psum_tensor(f"att{i}", [P, L], F32)) for i in range(4)]
        F = [ctx.enter_context(nc.psum_tensor(f"ffn{i}", [P, L], F32)) for i in range(4)]

        x_loaded = [sem(f"x_loaded{b}") for b in range(B)]
        kv_w_loaded = sem("kv_w_loaded")
        qg_w_loaded = sem("qg_w_loaded")
        gk_loaded = sem("gk_loaded")
        bias_hi_ready = sem("bias_hi_ready")
        bias_lo_ready = sem("bias_lo_ready")
        vecs_loaded = sem("vecs_loaded")
        vecs_turned = sem("vecs_turned")
        vecs_ready = sem("vecs_ready")
        wout_loaded = sem("wout_loaded")
        w12_loaded = sem("w12_loaded")
        h1_loaded = sem("h1_loaded")
        h2_loaded = sem("h2_loaded")
        w3_loaded = sem("w3_loaded")
        consts_zero = sem("consts_zero")
        consts_ready = sem("consts_ready")
        rep_ready = sem("rep_ready")
        proj_hi_ready = sem("proj_hi_ready")
        proj_lo_ready = sem("proj_lo_ready")
        gk1T_ready = sem("gk1T_ready")
        gk1T_copied = sem("gk1T_copied")
        gk12_ready = sem("gk12_ready")
        wT_ready = sem("wT_ready")
        wT_hi_ready = sem("wT_hi_ready")
        wT_lo_ready = sem("wT_lo_ready")
        lo_summed = sem("lo_summed")
        lo_any_ready = sem("lo_any_ready")
        lo_count_ready = sem("lo_count_ready")
        lo_flag_ready = sem("lo_flag_ready")
        wout_beta_ready = sem("wout_beta_ready")
        beta_part_ready = sem("beta_part_ready")
        beta_part_added = sem("beta_part_added")
        xT_ready = sem("xT_ready")
        x_hi_ready = sem("x_hi_ready")
        x_lo_ready = sem("x_lo_ready")
        kv_ready = sem("kv_ready")
        kv_copied = sem("kv_copied")
        z_ready = sem("z_ready")
        q_ready = sem("q_ready")
        g_ready = sem("g_ready")
        q_hi_ready = sem("q_hi_ready")
        q_lo_ready = sem("q_lo_ready")
        silu_g_ready = sem("silu_g_ready")
        z_abs_ready = sem("z_abs_ready")
        z_exp_ready = sem("z_exp_ready")
        z_ln_ready = sem("z_ln_ready")
        z_log_ready = sem("z_log_ready")
        gate_ready = sem("gate_ready")
        u_ready = sem("u_ready")
        uT_ready = sem("uT_ready")
        q_rep_ready = sem("q_rep_ready")
        scanned = sem("scanned")
        y_ready = sem("y_ready")
        summed = sem("summed")
        pair_ready = sem("pair_ready")
        o_ready = sem("o_ready")
        oT_ready = sem("oT_ready")
        o_stats_ready = sem("o_stats_ready")
        stats_seen = sem("stats_seen")
        o_mv_ready = sem("o_mv_ready")
        o_var_ready = sem("o_var_ready")
        o_rstd_ready = sem("o_rstd_ready")
        centered = sem("centered")
        gated = sem("gated")
        r_ready = sem("r_ready")
        x1_ready = sem("x1_ready")
        r_stats_ready = sem("r_stats_ready")
        r_mv_ready = sem("r_mv_ready")
        r_var_ready = sem("r_var_ready")
        r_rstd_ready = sem("r_rstd_ready")
        x2_ready = sem("x2_ready")
        x2T_ready = sem("x2T_ready")
        x2_kept = sem("x2_kept")
        x2_hi_ready = sem("x2_hi_ready")
        x2_lo_ready = sem("x2_lo_ready")
        a_ready = sem("a_ready")
        b_ready = sem("b_ready")
        silu_a_ready = sem("silu_a_ready")
        f1_ready = sem("f1_ready")
        f1_hi_ready = sem("f1_hi_ready")
        hid_ready = sem("hid_ready")
        gelu_hi_ready = sem("gelu_hi_ready")
        gelu_ready = sem("gelu_ready")
        dve_rested = sem("dve_rested")
        pool_rested = sem("pool_rested")
        w3_ready = sem("w3_ready")
        yT_ready = sem("yT_ready")
        y_tok_ready = sem("y_tok_ready")
        e_sum_ready = sem("e_sum_ready")
        e_stats_ready = sem("e_stats_ready")
        e_mv_ready = sem("e_mv_ready")
        e_var_ready = sem("e_var_ready")
        e_rstd_ready = sem("e_rstd_ready")
        e_minus_ready = sem("e_minus_ready")
        e_shift_ready = sem("e_shift_ready")
        out_ready = sem("out_ready")
        out_stored = sem("out_stored")

        x_rows = x.rearrange("b (j p) c -> b p j c", p=P)
        out_rows = out.rearrange("b (j p) c -> b p j c", p=P)

        def tile(j):
            return slice(j * P, (j + 1) * P)

        weight_banks = []
        for layer in range(2):
            weight_banks.append(([w12_raw[:, layer, o, :] for o in range(OB)],
                                 w12_hi[:, layer, :], w12_lo[:, layer, :], (w12_loaded, 32)))
        for layer, loaded in ((0, h1_loaded), (1, h2_loaded)):
            for c in range(OB):
                weight_banks.append(([h_raw[:, layer, o, tile(c)] for o in range(OB)],
                                     h_hi[:, layer, c, :], h_lo[:, layer, c, :], (loaded, 16)))
        weight_banks.append(([w3_raw[:, tile(c)] for c in range(OB)],
                             w3_hi[:, :, :].rearrange("p c d -> p (c d)"),
                             w3_lo[:, :, :].rearrange("p c d -> p (c d)"), (w3_loaded, 16)))
        WB = len(weight_banks)
        lo_groups = [(w12_lo[:].rearrange("p n d -> p (n d)"), 2)]
        for n in range(OB):
            lo_groups.append((h_lo[:, n // 2, 2 * (n % 2):2 * (n % 2) + 2].rearrange("p c d -> p (c d)"), 4 + 2 * n))
        lo_groups.append((w3_lo[:].rearrange("p c d -> p (c d)"), WB))

        ALL_BLOCKS = [(layer, o) for layer in range(3) for o in range(OB)]
        ON_POOL = [(0, 0), (0, 1), (0, 2), (1, 0), (1, 1)]
        ON_DVE = [n for n in ALL_BLOCKS if n not in ON_POOL]
        hidden = ((f1_hi, f1_lo), (f2_hi, f2_lo), (f1_hi, f1_lo))

        def rested(b, layer, o):
            side, order = (pool_rested, ON_POOL) if (layer, o) in ON_POOL else (dve_rested, ON_DVE)
            return side, len(order) * b + order.index((layer, o)) + 1

        def out_bank(layer, o):
            return F[((2 * o + 1) % 4, o, (o + 2) % 4)[layer]]

        def full_block(layer, o):
            if (layer, o) not in ON_POOL:
                return out_bank(layer, o)[:]
            return full[:, o % SLOTS]

        W3_BANK, Y_BANK = F[2], A[0]

        def q_bank(b, k):
            first_row = isinstance(b, int) and b == 0
            return A[k % 2 if first_row else 1 - k % 2]

        HALVES = (slice(0, L // 2), slice(L // 2, L))
        LAST_W3 = (F[2], F[3])
        LAST_Y = (A[0], A[1])

        X_BANK = (A[0], F[0], F[1], F[2])
        Z_BANK = (A[3], F[3], F[0], F[1])
        KV_BANKS = ((A[1], A[2]), (F[3], F[2]), (F[3], F[2]), (F[3], F[2]))
        Q_BANK = (A[0], F[0], F[0], F[0])
        G_BANK = (F[1], F[2], F[3], F[0])
        W_BANK = (A[0], A[1], A[1], A[1], F[1], F[1], F[2], F[3], F[0], F[1], F[2])
        U_ON_DVE, LATER_U_ON_DVE = (2, 3), 1

        block = ctx.enter_context(nc.Block())

        @block.sync
        def _(sp):
            sp.dma_start(x_tok[:, 0], x_rows[0]).then_inc(x_loaded[0], 16)
            for n, w in enumerate((Wk, Wv)):
                sp.dma_start(proj_raw[:, n, :], w).then_inc(kv_w_loaded, 16)
            sp.dma_start(wgk1[:], Wgk1).then_inc(gk_loaded, 16)
            sp.dma_start(wgk2[:], Wgk2).then_inc(gk_loaded, 16)
            sp.dma_start(bias_row[:], bgk2.rearrange("(o p) -> o p", p=P)).then_inc(gk_loaded, 16)
            for n, v in enumerate((w1_s, w2_s, h1_s, h2_s)):
                sp.dma_start(vec_rows[n * OB:(n + 1) * OB, :],
                             v.rearrange("(o p) -> o p", p=P)).then_inc(vecs_loaded, 16)
            for n, v in enumerate((w3_s, gamma, beta)):
                sp.dma_start(vec_rows[4 * OB + n:4 * OB + n + 1, :],
                             v.rearrange("(o p) -> o p", p=P)).then_inc(vecs_loaded, 16)
            sp.dma_start(x_tok[:, 1], x_rows[1]).then_inc(x_loaded[1], 16)
            for n, w in enumerate((Wq, Wg)):
                sp.dma_start(proj_raw[:, 2 + n, :], w).then_inc(qg_w_loaded, 16)
            for b in range(2, B):
                sp.dma_start(x_tok[:, b], x_rows[b]).then_inc(x_loaded[b], 16)
            for n, w in enumerate((w1_w, w2_w)):
                sp.dma_start(w12_raw[:, n], w.rearrange("(o p) c -> p o c", p=P)).then_inc(w12_loaded, 16)
            sp.dma_start(wout[:], Wout).then_inc(wout_loaded, 16)
            sp.dma_start(h_raw[:, 0], h1_w.rearrange("(o p) c -> p o c", p=P)).then_inc(h1_loaded, 16)
            sp.dma_start(h_raw[:, 1], h2_w.rearrange("(o p) c -> p o c", p=P)).then_inc(h2_loaded, 16)
            sp.dma_start(w3_raw[:], w3_w).then_inc(w3_loaded, 16)

            def store_out(b):
                sp.wait_ge(out_ready, TILES * (b + 1) + 1)
                sp.dma_start(out_rows[b], out_tok[:, b]).then_inc(out_stored, 16)

            with sp.Fori(0, B - 1) as b:
                store_out(b)
            for h in range(2):
                pair = slice(2 * h, 2 * h + 2)
                sp.wait_ge(out_ready, TILES * (B - 1) + 2 * (h + 1) + 1)
                sp.dma_start(out_rows[B - 1][:, pair], out_tok[:, B - 1, pair]).then_inc(out_stored, 16)
            sp.wait_ge(out_stored, 16 * (B + 1))

        @block.gpsimd
        def _(pool):
            nc.gpsimd.memset(ident[:], 0.0).then_inc(consts_zero, 1)
            nc.gpsimd.memset(rep_f[:], 0.0).then_inc(consts_zero, 1)
            nc.gpsimd.memset(center[:], -1.0 / P).then_inc(consts_zero, 1)
            pool.wait_ge(consts_zero, 1)
            nc.gpsimd.affine_select(out=ident[:], in_=ident[:], compare_op=ALU.not_equal, fill=1.0, base=0,
                                    pattern=[[-1, P]], channel_multiplier=1).then_inc(consts_ready, 1)
            pool.wait_ge(consts_zero, 2)
            rep_v = rep_f[:].rearrange("p k (h v) -> p k h v", v=DH)
            nc.gpsimd.affine_select(out=rep_v, in_=rep_v, compare_op=ALU.not_equal, fill=1.0, base=0,
                                    pattern=[[-1, DH], [-DH, HEADS], [0, DH]],
                                    channel_multiplier=1).then_inc(consts_ready, 1)
            nc.gpsimd.memset(half_neg[:], -0.5).then_inc(consts_ready, 1)
            nc.gpsimd.memset(eps[:], EPS).then_inc(consts_ready, 1)
            nc.gpsimd.memset(ones[:], 1.0).then_inc(consts_ready, 1)
            nc.gpsimd.memset(ones_f[:], 1.0).then_inc(consts_ready, 1)
            pool.wait_ge(consts_zero, 3)
            nc.gpsimd.affine_select(out=center[:], in_=center[:], compare_op=ALU.not_equal, fill=1.0 - 1.0 / P, base=0,
                                    pattern=[[-1, P]], channel_multiplier=1).then_inc(consts_ready, 1)
            pool.wait_ge(consts_ready, 7)

            def outer_products(b, tiles):
                for j in tiles:
                    if j == 0:
                        if not (isinstance(b, int) and b == 0):
                            pool.wait_ge(uT_ready, DH * b)
                    pool.wait_ge(kv_copied, 2 * b + j // 2 + 1)
                    k_b = kv_tok[:, b, j, 0:HID].rearrange("p (h k) -> p k h", k=DH)
                    v_b = kv_tok[:, b, j, HID:2 * HID].rearrange("p (h v) -> p h v", v=DH)
                    nc.gpsimd.tensor_tensor(
                        u_tok[:, j].rearrange("p k (h v) -> p k h v", v=DH),
                        v_b.unsqueeze(1).to_broadcast([P, DH, HEADS, DH]),
                        k_b.unsqueeze(3).to_broadcast([P, DH, HEADS, DH]), ALU.mult).then_inc(u_ready, 1)

            def sum_over_k(b, ks):
                for k in ks:
                    pool.wait_ge(y_ready, DH * b + k + 1)
                    if k == 1:
                        if not (isinstance(b, int) and b == 0):
                            pool.wait_ge(oT_ready, b)
                        first = y[:, 0]
                    else:
                        pool.wait_ge(summed, (DH - 3) * b + k - 1)
                        first = o_acc[:]
                    nc.gpsimd.tensor_tensor(o_acc[:], first, y[:, k % 4], ALU.add).then_inc(summed, 1)

            def rstd_of(b, var, var_ready, rstd, rstd_ready):
                pool.wait_ge(var_ready, b + 1)
                nc.gpsimd.tensor_tensor(rstd[:], var[:], half_neg[:], ALU.pow).then_inc(rstd_ready, 1)

            def o_rstd_of(b):
                rstd_of(b, o_var, o_var_ready, o_rstd, o_rstd_ready)

            def r_rstd_of(b):
                rstd_of(b, r_var, r_var_ready, r_rstd, r_rstd_ready)

            def e_rstd_of(b):
                rstd_of(b, e_var, e_var_ready, e_rstd, e_rstd_ready)
                pool.wait_ge(e_rstd_ready, b + 1)
                pool.wait_ge(e_minus_ready, b + 1)
                pool.wait_ge(out_ready, TILES * b + 1)
                nc.gpsimd.tensor_tensor(e_shift[:], e_minus[:], e_rstd[:], ALU.mult).then_inc(e_shift_ready, 1)

            def rest(b, layer, o):
                if layer == 0:
                    pool.wait_ge(f1_hi_ready, OB * b + o + 1)
                    pool.wait_ge(f1_ready, OB * b + o + 1)
                else:
                    pool.wait_ge(gelu_ready, 2 * OB * b + OB * (layer - 1) + o + 1)
                hi, lo = hidden[layer]
                nc.gpsimd.tensor_tensor(lo[:, o], full_block(layer, o), hi[:, o].bitcast(F32),
                                        ALU.subtract).then_inc(pool_rested, 1)

            def first_layer(b, follows):
                rest(b, 0, 0)
                rest(b, 0, 1)
                rest(b, 0, 2)
                if follows:
                    sum_over_k(b + 1, (1, 2))

            def attention_end(a, tiles, follows):
                if follows:
                    outer_products(a + 1, (0,))
                o_rstd_of(a)
                if follows:
                    outer_products(a + 1, tiles)
                r_rstd_of(a)
                if follows:
                    outer_products(a + 1, (3,))

            def ffn_middle(b, f, follows):
                if follows:
                    sum_over_k(b + 1, range(3, DH - 2))
                rest(b, 1, 0)
                rest(b, 1, 1)
                if f is not None:
                    e_rstd_of(f)

            outer_products(0, [j for j in range(TILES) if j not in U_ON_DVE])
            sum_over_k(0, range(1, DH - 2))
            attention_end(0, (1, 2), True)
            first_layer(0, True)
            ffn_middle(0, None, True)
            with pool.Fori(0, B - 2) as i:
                attention_end(i + 1, (2,), True)
                first_layer(i + 1, True)
                ffn_middle(i + 1, i, True)
            attention_end(B - 1, (), False)
            first_layer(B - 1, False)
            ffn_middle(B - 1, B - 2, False)
            for h in range(2):
                pair = slice(2 * h, 2 * h + 2)
                pool.wait_ge(e_var_ready, B + h)
                nc.gpsimd.tensor_tensor(e_rstd[:, pair], e_var[:, pair], half_neg[:, pair],
                                        ALU.pow).then_inc(e_rstd_ready, 1)
                pool.wait_ge(e_rstd_ready, B + h)
                pool.wait_ge(e_minus_ready, B + h)
                pool.wait_ge(out_ready, TILES * (B - 1) + 1)
                nc.gpsimd.tensor_tensor(e_shift[:, pair], e_minus[:, pair], e_rstd[:, pair],
                                        ALU.mult).then_inc(e_shift_ready, 1)

        @block.tensor
        def _(pe):
            def three_passes(ps, wh, wl, mh, ml, start=True, stop=True, before_lo=None):
                nc.tensor.matmul(ps, wh, mh, start=start, stop=False)
                nc.tensor.matmul(ps, wl, mh, start=False, stop=False)
                if before_lo is not None:
                    pe.wait_ge(*before_lo)
                return nc.tensor.matmul(ps, wh, ml, start=False, stop=stop)

            def transpose_x(b):
                pe.wait_ge(x_loaded[b], 16)
                for j in range(TILES):
                    last = nc.tensor.transpose(X_BANK[b][:, tile(j)], x_tok[:, b, j, :], ident[:])
                last.then_inc(xT_ready, 1)

            def project_kv(b):
                if b == 0:
                    pe.wait_ge(x_hi_ready, 1)
                    pe.wait_ge(x_lo_ready, 1)
                    pe.wait_ge(proj_lo_ready, 1)
                kv_h = proj_hi[:, 0:2, :].rearrange("p n c -> p (n c)")
                kv_l = proj_lo[:, 0:2, :].rearrange("p n c -> p (n c)")
                for pair in range(2):
                    if b == 1:
                        pe.wait_ge(*((z_log_ready, 2), (x_lo_ready, 4))[pair])
                    elif b >= 2:
                        pe.wait_ge(kv_copied, 2 * (b - 1) + pair + 1)
                    for half in range(2):
                        t = tile(2 * pair + half)
                        ps = KV_BANKS[b][pair][:, half * 2 * HID:(half + 1) * 2 * HID]
                        nc.tensor.matmul(ps, x_hi[:, b, t], kv_h, start=True, stop=False)
                        nc.tensor.matmul(ps, x_hi[:, b, t], kv_l, start=False, stop=False)
                        last = nc.tensor.matmul(ps, x_lo[:, b, t], kv_h, start=False, stop=True)
                    last.then_inc(kv_ready, 1)

            def project(b, n, bank, ready):
                three_passes(bank[:], proj_hi[:, n], proj_lo[:, n], x_hi[:, b], x_lo[:, b]).then_inc(ready, 1)

            def project_z(b):
                pe.wait_ge(proj_lo_ready, 2)
                pe.wait_ge(x_lo_ready, b + 1)
                pe.wait_ge(bias_hi_ready, 2)
                pe.wait_ge(bias_lo_ready, 1)
                bank = Z_BANK[b][:]
                nc.tensor.matmul(bank, bias_hi[:], ones_row[:], start=True, stop=False)
                nc.tensor.matmul(bank, bias_lo[:], ones_row[:], start=False, stop=False)
                three_passes(bank, proj_hi[:, 4], proj_lo[:, 4], x_hi[:, b], x_lo[:, b],
                             start=False).then_inc(z_ready, 1)

            def project_q(b):
                pe.wait_ge(proj_lo_ready, 3)
                if b == 1:
                    pe.wait_ge(z_log_ready, 3)
                elif b >= 2:
                    pe.wait_ge(q_lo_ready, b)
                project(b, 2, Q_BANK[b], q_ready)

            def project_g(b):
                pe.wait_ge(*((z_log_ready, 4), (kv_copied, 2 * B), (kv_copied, 2 * B - 1), (q_lo_ready, B))[b])
                project(b, 3, G_BANK[b], g_ready)

            def replicate_q(b, k):
                if k == 0:
                    if isinstance(b, int) and b == 0:
                        pe.wait_ge(q_lo_ready, 1)
                    else:
                        pe.wait_ge(x2_lo_ready, b)
                elif k == 1:
                    if isinstance(b, int) and b == 0:
                        pe.wait_ge(kv_copied, 1)
                    else:
                        pe.wait_ge(x2_ready, TILES * b)
                        pe.wait_ge(e_sum_ready, b)
                else:
                    pe.wait_ge(y_ready, DH * b + k - 1)
                nc.tensor.matmul(q_bank(b, k)[:], rep[:, k], q_hi[:, b], start=True, stop=False)
                nc.tensor.matmul(q_bank(b, k)[:], rep[:, k], q_lo[:, b], start=False, stop=True).then_inc(q_rep_ready, 1)

            def transpose_u(b, k):
                if k == 0:
                    pe.wait_ge(u_ready, TILES * (b + 1))
                    if not (isinstance(b, int) and b == 0):
                        pe.wait_ge(o_stats_ready, TILES * b)
                elif k == 1:
                    if isinstance(b, int) and b == 0:
                        pe.wait_ge(z_log_ready, 1)
                    else:
                        pe.wait_ge(gated, b)
                else:
                    pe.wait_ge(scanned, DH * b + k - 1)
                for j in range(TILES):
                    last = nc.tensor.transpose(A[2 + k % 2][:, tile(j)], u_tok[:, j, k], ident[:])
                last.then_inc(uT_ready, 1)

            def transpose_o(b):
                pe.wait_ge(o_ready, b + 1)
                for j in range(TILES):
                    last = nc.tensor.transpose(A[2][:, tile(j)], o_acc[:, tile(j)], ident[:])
                last.then_inc(oT_ready, 1)

            def center_o(b):
                pe.wait_ge(o_ready, b + 1)
                nc.tensor.matmul(A[3][:], center[:], o_acc[:], start=True, stop=True).then_inc(centered, 1)

            def project_beta(b):
                pe.wait_ge(silu_g_ready, b + 1)
                pe.wait_ge(wout_beta_ready, 1)
                for j in range(TILES):
                    last = nc.tensor.matmul(G_BANK[b][:, tile(j)], silu_g[:, b, tile(j)], wout_beta[:],
                                            start=True, stop=True)
                last.then_inc(beta_part_ready, 1)

            def project_out(b):
                pe.wait_ge(gated, b + 1)
                if isinstance(b, int) and b == 0:
                    pe.wait_ge(wT_lo_ready, 1)
                for j in range(TILES):
                    last = nc.tensor.matmul(A[0][:, tile(j)], og[:, tile(j)], wout[:], start=True, stop=True)
                last.then_inc(r_ready, 1)

            def transpose_x2(b):
                if isinstance(b, int) and b == 0:
                    pe.wait_ge(wT_lo_ready, 4)
                for j in range(TILES):
                    pe.wait_ge(x2_ready, TILES * b + j + 1)
                    last = nc.tensor.transpose(A[1][:, tile(j)], x2[:, j], ident[:])
                last.then_inc(x2T_ready, 1)

            def bank_read(b, layer, o):
                if layer == 0:
                    pe.wait_ge(f1_ready, OB * b + o + 1)
                else:
                    pe.wait_ge(gelu_ready, 2 * OB * b + OB * (layer - 1) + o + 1)
                if (layer, o) not in ON_POOL:
                    pe.wait_ge(*rested(b, layer, o))

            def ffn_in(b, o, with_lo):
                if o == 0:
                    pe.wait_ge(x2_hi_ready, b + 1)
                if o == 1:
                    pe.wait_ge(yT_ready, b + 1)
                if o >= 2:
                    pe.wait_ge(silu_a_ready, OB * b + o - 1)
                for n, ready in ((0, a_ready), (1, b_ready)):
                    bank = F[(2 * o + n) % 4]
                    if n == 1 and o >= 2:
                        bank_read(b, 0, o - 2)
                    nc.tensor.matmul(bank[:], w12_hi[:, n, tile(o)], x2_hi[:], start=True, stop=False)
                    if with_lo:
                        nc.tensor.matmul(bank[:], w12_lo[:, n, tile(o)], x2_hi[:], start=False, stop=False)
                    if o == 0 and n == 0:
                        pe.wait_ge(x2_lo_ready, b + 1)
                    nc.tensor.matmul(bank[:], w12_hi[:, n, tile(o)], x2_lo[:], start=False,
                                     stop=True).then_inc(ready, 1)

            def ffn_hidden(b, layer, o, with_lo):
                src_hi = hidden[layer - 1][0]
                bank = out_bank(layer, o)
                if layer == 1 and o in (0, 2):
                    pe.wait_ge(silu_a_ready, OB * b + OB - 1 + o // 2)
                elif layer == 1:
                    bank_read(b, 0, OB - 2 + o // 2)
                else:
                    bank_read(b, 1, (o + 2) % OB)
                for c in range(OB):
                    if layer == 1:
                        pe.wait_ge(f1_hi_ready, OB * b + c + 1)
                    else:
                        pe.wait_ge(gelu_hi_ready, 2 * OB * b + c + 1)
                    nc.tensor.matmul(bank[:], h_hi[:, layer - 1, c, tile(o)], src_hi[:, c],
                                     start=(c == 0), stop=False)
                    if with_lo:
                        nc.tensor.matmul(bank[:], h_lo[:, layer - 1, c, tile(o)], src_hi[:, c],
                                         start=False, stop=False)

            def ffn_hidden_rest(b, layer, o):
                for c in range(OB):
                    pe.wait_ge(*rested(b, layer - 1, c))
                    last = nc.tensor.matmul(out_bank(layer, o)[:], h_hi[:, layer - 1, c, tile(o)],
                                            hidden[layer - 1][1][:, c], start=False, stop=(c == OB - 1))
                last.then_inc(hid_ready, 1)

            def ffn_out_hi(b, with_lo):
                bank_read(b, 2, 0)
                for c in range(OB):
                    pe.wait_ge(gelu_hi_ready, 2 * OB * b + OB + c + 1)
                    nc.tensor.matmul(W3_BANK[:], w3_hi[:, c], f1_hi[:, c], start=(c == 0), stop=False)
                    if with_lo:
                        nc.tensor.matmul(W3_BANK[:], w3_lo[:, c], f1_hi[:, c], start=False, stop=False)

            def ffn_out_rest(b):
                for c in range(OB):
                    pe.wait_ge(*rested(b, 2, c))
                    last = nc.tensor.matmul(W3_BANK[:], w3_hi[:, c], f1_lo[:, c], start=False, stop=(c == OB - 1))
                last.then_inc(w3_ready, 1)

            def last_out(with_lo):
                b = B - 1
                for h, half in enumerate(HALVES):
                    bank_read(b, 2, h)
                    for c in range(OB):
                        pe.wait_ge(gelu_hi_ready, 2 * OB * b + OB + c + 1)
                        nc.tensor.matmul(LAST_W3[h][:, half], w3_hi[:, c], f1_hi[:, c, half], start=(c == 0), stop=False)
                        if with_lo:
                            nc.tensor.matmul(LAST_W3[h][:, half], w3_lo[:, c], f1_hi[:, c, half], start=False, stop=False)
                    for c in range(OB):
                        pe.wait_ge(*rested(b, 2, c))
                        last = nc.tensor.matmul(LAST_W3[h][:, half], w3_hi[:, c], f1_lo[:, c, half], start=False,
                                                stop=(c == OB - 1))
                    last.then_inc(w3_ready, 1)
                for h in range(2):
                    pe.wait_ge(yT_ready, b + 2 + h)
                    for j in (2 * h, 2 * h + 1):
                        last = nc.tensor.transpose(LAST_Y[h][:, tile(j)], yT[:, tile(j)], ident[:])
                    last.then_inc(y_tok_ready, 1)

            def transpose_y(b):
                pe.wait_ge(yT_ready, b + 2)
                for j in range(TILES):
                    last = nc.tensor.transpose(Y_BANK[:, tile(j)], yT[:, tile(j)], ident[:])
                last.then_inc(y_tok_ready, 1)

            def weight_bank(n):
                blocks, _, _, loaded = weight_banks[n]
                pe.wait_ge(*loaded)
                pe.wait_ge(*((y_ready, DH - 1), (y_ready, DH), (wT_lo_ready, 2), (wT_lo_ready, 3),
                             (beta_part_added, 1), (wT_lo_ready, 5), (beta_part_added, 2), (beta_part_added, 3),
                             (beta_part_added, 4), (wT_lo_ready, 6), (wT_lo_ready, 7))[n])
                for j, w in enumerate(blocks):
                    last = nc.tensor.transpose(W_BANK[n][:, tile(j)], w, ident[:])
                last.then_inc(wT_ready, 1)

            def count_lo():
                pe.wait_ge(lo_any_ready, 1)
                pe.wait_ge(y_ready, DH + 1)
                for n in range(len(lo_groups)):
                    last = nc.tensor.matmul(A[1][0:1, 0:1], lo_any[:, n:n + 1], ones[:], start=(n == 0),
                                            stop=(n == len(lo_groups) - 1))
                last.then_inc(lo_count_ready, 1)

            def first_layer(b, f, with_lo, follows):
                if follows:
                    transpose_u(b + 1, 0)
                    transpose_u(b + 1, 1)
                    replicate_q(b + 1, 0)
                ffn_in(b, 0, with_lo)
                ffn_in(b, 1, with_lo)
                if f is not None:
                    transpose_y(f)
                ffn_in(b, 2, with_lo)
                if follows:
                    transpose_u(b + 1, 2)
                ffn_in(b, 3, with_lo)
                if follows:
                    replicate_q(b + 1, 1)
                    replicate_q(b + 1, 2)
                    transpose_u(b + 1, 3)

            def step(a, f, with_lo, follows):
                transpose_u(a, 4)
                ffn_hidden(f, 1, 0, with_lo)
                replicate_q(a, 3)
                ffn_hidden_rest(f, 1, 0)
                transpose_u(a, 5)
                replicate_q(a, 4)
                ffn_hidden(f, 1, 1, with_lo)
                transpose_u(a, 6)
                replicate_q(a, 5)
                ffn_hidden_rest(f, 1, 1)
                transpose_u(a, 7)
                replicate_q(a, 6)
                ffn_hidden(f, 1, 2, with_lo)
                replicate_q(a, 7)
                ffn_hidden_rest(f, 1, 2)
                ffn_hidden(f, 1, 3, with_lo)
                ffn_hidden_rest(f, 1, 3)
                center_o(a)
                transpose_o(a)
                ffn_hidden(f, 2, 0, with_lo)
                project_out(a)
                ffn_hidden_rest(f, 2, 0)
                ffn_hidden(f, 2, 1, with_lo)
                ffn_hidden_rest(f, 2, 1)
                ffn_hidden(f, 2, 2, with_lo)
                ffn_hidden_rest(f, 2, 2)
                ffn_hidden(f, 2, 3, with_lo)
                ffn_hidden_rest(f, 2, 3)
                ffn_out_hi(f, with_lo)
                transpose_x2(a)
                ffn_out_rest(f)
                first_layer(a, f, with_lo, follows)

            def rows(with_lo):
                with pe.Fori(0, B - 2) as i:
                    step(i + 1, i, with_lo, True)
                step(B - 1, B - 2, with_lo, False)
                for layer in (1, 2):
                    for o in range(OB):
                        ffn_hidden(B - 1, layer, o, with_lo)
                        ffn_hidden_rest(B - 1, layer, o)
                last_out(with_lo)

            pe.wait_ge(consts_ready, 1)
            transpose_x(0)
            pe.wait_ge(gk_loaded, 48)
            nc.tensor.transpose(A[3][0:RANK, 0:P], wgk1[:], ident[:]).then_inc(gk1T_ready, 1)
            pe.wait_ge(gk1T_copied, 1)
            nc.tensor.matmul(A[3][:, P:2 * P], wgk1T[:], wgk2[:], start=True, stop=True).then_inc(gk12_ready, 1)
            project_kv(0)
            pe.wait_ge(vecs_loaded, 16 * 7)
            nc.tensor.transpose(F[3][:, 0:VECS], vec_rows[:], ident[0:VECS, 0:VECS]).then_inc(vecs_turned, 1)
            project_z(0)
            project_q(0)
            transpose_x(1)
            transpose_u(0, 0)
            transpose_u(0, 1)
            pe.wait_ge(rep_ready, 1)
            replicate_q(0, 0)
            replicate_q(0, 1)
            transpose_x(2)
            pe.wait_ge(vecs_ready, 1)
            project_z(1)
            transpose_u(0, 2)
            replicate_q(0, 2)
            transpose_x(3)
            for k in range(3, DH):
                transpose_u(0, k)
                replicate_q(0, k)
                if k == 3:
                    project_z(2)
                elif k == 4:
                    project_z(3)
                elif k == 5:
                    project_kv(1)
                elif k == 6:
                    project_q(1)
            weight_bank(0)
            project_g(0)
            project_kv(2)
            weight_bank(1)
            project_q(2)
            transpose_o(0)
            center_o(0)
            project_beta(0)
            project_kv(3)
            project_out(0)
            project_q(3)
            weight_bank(2)
            project_g(1)
            project_g(2)
            weight_bank(3)
            project_g(3)
            weight_bank(4)
            project_beta(1)
            project_beta(2)
            transpose_x2(0)
            project_beta(3)
            weight_bank(5)
            weight_bank(6)
            transpose_u(1, 0)
            weight_bank(7)
            weight_bank(8)
            transpose_u(1, 1)
            weight_bank(9)
            weight_bank(10)
            replicate_q(1, 0)
            replicate_q(1, 1)
            pe.wait_ge(wT_lo_ready, WB - 1)
            ffn_in(0, 0, True)
            pe.wait_ge(wT_lo_ready, WB)
            ffn_in(0, 1, True)
            transpose_u(1, 2)
            ffn_in(0, 2, True)
            ffn_in(0, 3, True)
            count_lo()
            transpose_u(1, 3)
            pe.wait_ge(lo_flag_ready, 1)
            replicate_q(1, 2)
            has_lo = pe.value_load(lo_flag[0:1, 0:1], min_val=0, max_val=1)
            with pe.If(has_lo):
                rows(True)
            with pe.Else():
                rows(False)

        @block.scalar
        def _(act):
            def round_x(b):
                act.wait_ge(xT_ready, b + 1)
                nc.scalar.copy(x_hi[:, b], X_BANK[b][:]).then_inc(x_hi_ready, 1)

            def copy_kv(b):
                for pair in range(2):
                    act.wait_ge(kv_ready, 2 * b + pair + 1)
                    nc.scalar.copy(kv_tok[:, b, 2 * pair:2 * pair + 2, :].rearrange("p j c -> p (j c)"),
                                   KV_BANKS[b][pair][:]).then_inc(kv_copied, 1)

            def round_q(b):
                act.wait_ge(q_ready, b + 1)
                nc.scalar.copy(q_hi[:, b], Q_BANK[b][:]).then_inc(q_hi_ready, 1)

            def log_part(b):
                act.wait_ge(z_ready, b + 1)
                if b >= 2:
                    act.wait_ge(z_log_ready, b - 1)
                z = z_a[:, b % 2]
                nc.scalar.activation(z, Z_BANK[b][:], ACT.Abs).then_inc(z_abs_ready, 1)
                act.wait_ge(z_abs_ready, b + 1)
                nc.scalar.activation(z, z, ACT.Exp, scale=-1.0).then_inc(z_exp_ready, 1)
                act.wait_ge(z_exp_ready, b + 1)
                nc.scalar.activation(z, z, ACT.Ln, bias=1.0).then_inc(z_ln_ready, 1)

            def gates(b):
                act.wait_ge(z_log_ready, b + 1)
                nc.scalar.activation(gate[:, b], gate[:, b], ACT.Exp, scale=GATE_SCALE).then_inc(gate_ready, 1)

            def silu_of_g(b):
                act.wait_ge(g_ready, b + 1)
                nc.scalar.activation(silu_g[:, b], G_BANK[b][:], ACT.Silu).then_inc(silu_g_ready, 1)

            def fold_beta():
                act.wait_ge(wout_loaded, 16)
                nc.scalar.activation(wout_beta[:], wout[:], ACT.Identity, scale=beta_col).then_inc(wout_beta_ready, 1)

            def keep_x2(b):
                act.wait_ge(x2_ready, TILES * (b + 1))
                nc.scalar.copy(x_tok[:, b], x2[:]).then_inc(x2_kept, 1)

            def round_x2(b):
                act.wait_ge(x2T_ready, b + 1)
                if not (isinstance(b, int) and b == 0):
                    act.wait_ge(b_ready, OB * b)
                nc.scalar.copy(x2_hi[:], A[1][:]).then_inc(x2_hi_ready, 1)

            def ffn_silu(b, o):
                act.wait_ge(a_ready, OB * b + o + 1)
                if o >= SLOTS:
                    act.wait_ge(f1_ready, OB * b + o - SLOTS + 1)
                    if (0, o - SLOTS) in ON_POOL:
                        act.wait_ge(*rested(b, 0, o - SLOTS))
                nc.scalar.activation(full[:, o % SLOTS], F[(2 * o) % 4][:], ACT.Silu,
                                     scale=scales[:, 0, o:o + 1]).then_inc(silu_a_ready, 1)

            def ffn_round(b, o):
                act.wait_ge(f1_ready, OB * b + o + 1)
                nc.scalar.copy(f1_hi[:, o], full_block(0, o)).then_inc(f1_hi_ready, 1)

            def ffn_gelu(b, layer, o):
                n = 2 * OB * b + OB * (layer - 1) + o + 1
                if layer == 2 and o == 0:
                    act.wait_ge(hid_ready, 2 * OB * b + OB)
                act.wait_ge(hid_ready, n)
                bank = out_bank(layer, o)
                nc.scalar.activation(hidden[layer][0][:, o], bank[:], ACT.Gelu,
                                     scale=scales[:, 1 + layer, o:o + 1]).then_inc(gelu_hi_ready, 1)
                act.wait_ge(gelu_hi_ready, n)
                nc.scalar.activation(full_block(layer, o), bank[:], ACT.Gelu,
                                     scale=scales[:, 1 + layer, o:o + 1]).then_inc(gelu_ready, 1)

            def scale_y(b):
                act.wait_ge(w3_ready, b + 1)
                nc.scalar.activation(yT[:], W3_BANK[:], ACT.Identity, scale=w3_col).then_inc(yT_ready, 1)

            def out_normalise(b):
                act.wait_ge(e_rstd_ready, b + 1)
                act.wait_ge(e_shift_ready, b + 1)
                for j in range(TILES):
                    nc.scalar.activation(out_tok[:, b, j], out_tok[:, b, j], ACT.Identity, scale=e_rstd[:, j:j + 1],
                                         bias=e_shift[:, j:j + 1]).then_inc(out_ready, 1)

            def sum_lo(n):
                if n == 0:
                    scratch = full[:, 0:2].rearrange("p n t -> p (n t)")
                else:
                    scratch = lo_abs[:]
                    act.wait_ge(g_ready, B)
                lo, banks = lo_groups[n]
                act.wait_ge(wT_lo_ready, banks)
                if n >= 1:
                    act.wait_ge(lo_summed, n)
                nc.scalar.activation(scratch[:, 0:lo.shape[1]], lo.bitcast(F32), ACT.Abs,
                                     accum_out=lo_sums[:, n:n + 1]).then_inc(lo_summed, 1)

            def weight_bank_hi(n):
                act.wait_ge(wT_ready, n + 1)
                nc.scalar.copy(weight_banks[n][1], W_BANK[n][:]).then_inc(wT_hi_ready, 1)

            def first_layer(b, f, out_too):
                for o in range(OB):
                    ffn_silu(b, o)
                    if o >= 1:
                        ffn_round(b, o - 1)
                ffn_round(b, OB - 1)
                nc.scalar.preload_act_table_set(GELU_SET)
                keep_x2(b)
                for o in range(OB):
                    ffn_gelu(b, 1, o)
                if out_too:
                    out_normalise(f)

            def step(a, f, out_too):
                ffn_gelu(f, 2, 0)
                ffn_gelu(f, 2, 1)
                ffn_gelu(f, 2, 2)
                ffn_gelu(f, 2, 3)
                round_x2(a)
                nc.scalar.preload_act_table_set(SILU_SET)
                scale_y(f)
                first_layer(a, f, out_too)

            nc.scalar.preload_act_table_set("natural_log_exp_and_others")
            round_x(0)
            act.wait_ge(kv_w_loaded, 32)
            nc.scalar.copy(proj_hi[:, 0:2], proj_raw[:, 0:2]).then_inc(proj_hi_ready, 1)
            act.wait_ge(gk1T_ready, 1)
            nc.scalar.copy(wgk1T[:], A[3][0:RANK, 0:P]).then_inc(gk1T_copied, 1)
            act.wait_ge(gk12_ready, 1)
            nc.scalar.copy(proj_hi[:, 4], A[3][:, P:2 * P]).then_inc(proj_hi_ready, 1)
            act.wait_ge(gk_loaded, 48)
            nc.scalar.copy(bias_hi[:], bias_row[:]).then_inc(bias_hi_ready, 1)
            act.wait_ge(consts_ready, 7)
            nc.scalar.copy(ones_row[:], ones_f[:]).then_inc(bias_hi_ready, 1)
            nc.scalar.copy(rep[:], rep_f[:]).then_inc(rep_ready, 1)
            copy_kv(0)
            act.wait_ge(vecs_turned, 1)
            nc.scalar.copy(vec_cols[:], F[3][:, 0:VECS]).then_inc(vecs_ready, 1)
            act.wait_ge(qg_w_loaded, 32)
            nc.scalar.copy(proj_hi[:, 2:4], proj_raw[:, 2:4]).then_inc(proj_hi_ready, 1)
            act.wait_ge(vecs_ready, 1)
            log_part(0)
            round_q(0)
            round_x(1)
            gates(0)
            round_x(2)
            log_part(1)
            round_x(3)
            gates(1)
            log_part(2)
            log_part(3)
            gates(2)
            copy_kv(1)
            round_q(1)
            gates(3)
            weight_bank_hi(0)
            nc.scalar.preload_act_table_set(SILU_SET)
            silu_of_g(0)
            fold_beta()
            weight_bank_hi(1)
            copy_kv(2)
            round_q(2)
            copy_kv(3)
            round_q(3)
            weight_bank_hi(2)
            silu_of_g(1)
            silu_of_g(2)
            sum_lo(0)
            weight_bank_hi(3)
            silu_of_g(3)
            weight_bank_hi(4)
            round_x2(0)
            sum_lo(1)
            weight_bank_hi(5)
            weight_bank_hi(6)
            weight_bank_hi(7)
            sum_lo(2)
            weight_bank_hi(8)
            weight_bank_hi(9)
            sum_lo(3)
            weight_bank_hi(10)
            ffn_silu(0, 0)
            sum_lo(4)
            ffn_silu(0, 1)
            ffn_round(0, 0)
            sum_lo(5)
            ffn_silu(0, 2)
            ffn_round(0, 1)
            ffn_silu(0, 3)
            act.wait_ge(lo_summed, len(lo_groups))
            ffn_round(0, 2)
            ffn_round(0, 3)
            nc.scalar.preload_act_table_set(GELU_SET)
            keep_x2(0)
            for o in range(OB):
                ffn_gelu(0, 1, o)

            with act.Fori(0, B - 2) as i:
                step(i + 1, i, True)
            step(B - 1, B - 2, False)

            last_row = B - 1
            out_normalise(B - 2)
            for o in range(OB):
                ffn_gelu(last_row, 2, o)
            for h, half in enumerate(HALVES):
                act.wait_ge(w3_ready, B + h)
                nc.scalar.activation(yT[:, half], LAST_W3[h][:, half], ACT.Identity, scale=w3_col).then_inc(yT_ready, 1)
            for h in range(2):
                act.wait_ge(e_rstd_ready, B + h)
                act.wait_ge(e_shift_ready, B + h)
                for j in (2 * h, 2 * h + 1):
                    nc.scalar.activation(out_tok[:, last_row, j], out_tok[:, last_row, j], ACT.Identity,
                                         scale=e_rstd[:, j:j + 1], bias=e_shift[:, j:j + 1]).then_inc(out_ready, 1)

        @block.vector
        def _(dve):
            def rest_of_x(b):
                dve.wait_ge(x_hi_ready, b + 1)
                nc.vector.tensor_tensor(x_lo[:, b], X_BANK[b][:], x_hi[:, b].bitcast(F32),
                                        ALU.subtract).then_inc(x_lo_ready, 1)

            def outer_product(b, j):
                dve.wait_ge(kv_copied, 2 * b + j // 2 + 1)
                if not (isinstance(b, int) and b == 0):
                    dve.wait_ge(uT_ready, DH * b)
                k_b = kv_tok[:, b, j, 0:HID].rearrange("p (h k) -> p k h", k=DH)
                v_b = kv_tok[:, b, j, HID:2 * HID].rearrange("p (h v) -> p h v", v=DH)
                nc.vector.tensor_tensor(
                    u_tok[:, j].rearrange("p k (h v) -> p k h v", v=DH),
                    v_b.unsqueeze(1).to_broadcast([P, DH, HEADS, DH]),
                    k_b.unsqueeze(3).to_broadcast([P, DH, HEADS, DH]), ALU.mult).then_inc(u_ready, 1)

            def log_gate(b):
                dve.wait_ge(z_ln_ready, b + 1)
                nc.vector.scalar_tensor_tensor(gate[:, b], Z_BANK[b][:], 0.0, z_a[:, b % 2], ALU.min,
                                               ALU.subtract).then_inc(z_log_ready, 1)

            def rest_of_q(b):
                dve.wait_ge(q_hi_ready, b + 1)
                nc.vector.tensor_tensor(q_lo[:, b], Q_BANK[b][:], q_hi[:, b].bitcast(F32),
                                        ALU.subtract).then_inc(q_lo_ready, 1)

            def scan(b, k):
                dve.wait_ge(uT_ready, DH * b + k + 1)
                if k == 0:
                    dve.wait_ge(gate_ready, b + 1)
                if k >= 3:
                    dve.wait_ge(y_ready, DH * b + k - 2)
                elif not (isinstance(b, int) and b == 0):
                    dve.wait_ge(y_ready, DH * b)
                nc.vector.tensor_tensor_scan(state[:, k % 3], gate[:, b], A[2 + k % 2][:], 0.0,
                                             ALU.mult, ALU.add).then_inc(scanned, 1)

            def read_out(b, k):
                dve.wait_ge(q_rep_ready, DH * b + k + 1)
                dve.wait_ge(scanned, DH * b + k + 1)
                if k >= 4:
                    dve.wait_ge(summed, (DH - 3) * b + max(k - 4, 1))
                elif not (isinstance(b, int) and b == 0):
                    dve.wait_ge(summed, (DH - 3) * b)
                    dve.wait_ge(o_ready, b)
                nc.vector.tensor_tensor(y[:, k % 4], q_bank(b, k)[:], state[:, k % 3], ALU.mult).then_inc(y_ready, 1)

            def last_sums(b):
                dve.wait_ge(y_ready, DH * (b + 1))
                nc.vector.tensor_tensor(y[:, 3], y[:, 2], y[:, 3], ALU.add).then_inc(pair_ready, 1)
                dve.wait_ge(summed, (DH - 3) * (b + 1))
                dve.wait_ge(pair_ready, b + 1)
                nc.vector.tensor_tensor(o_acc[:], o_acc[:], y[:, 3], ALU.add).then_inc(o_ready, 1)

            def token_stats(b, bank, stats, stats_ready):
                for j in range(TILES):
                    nc.vector.bn_stats(stats[:, j], bank[:, tile(j)]).then_inc(stats_ready, 1)

            def mean_and_variance(b, stats, stats_ready, mv, mv_ready, var, var_ready):
                dve.wait_ge(stats_ready, TILES * (b + 1))
                dve.sem_inc(stats_seen, 1)
                for j in range(TILES):
                    nc.vector.bn_aggr(mv[:, j], stats[:, j]).then_inc(mv_ready, 1)
                dve.wait_ge(mv_ready, TILES * (b + 1))
                nc.vector.tensor_tensor(var[:], mv[:, :, 1], eps[:], ALU.add).then_inc(var_ready, 1)

            def normalise(dst, dst_ready, bank, mv, rstd):
                for j in range(TILES):
                    nc.vector.tensor_scalar(dst[:, j], bank[:, tile(j)], mv[:, j, 0:1], rstd[:, j:j + 1],
                                            ALU.subtract, ALU.mult).then_inc(dst_ready, 1)

            def o_token_stats(b):
                dve.wait_ge(oT_ready, b + 1)
                token_stats(b, A[2], o_stats, o_stats_ready)

            def o_mean_and_variance(b):
                mean_and_variance(b, o_stats, o_stats_ready, o_mv, o_mv_ready, o_var, o_var_ready)

            def add_beta_part(b):
                dve.wait_ge(beta_part_ready, b + 1)
                row = x_tok[:, b].rearrange("p j c -> p (j c)")
                nc.vector.tensor_tensor(row, G_BANK[b][:], row, ALU.add).then_inc(beta_part_added, 1)

            def apply_gate(b):
                dve.wait_ge(centered, b + 1)
                if isinstance(b, int) and b == 0:
                    dve.wait_ge(silu_g_ready, 1)
                if not (isinstance(b, int) and b == 0):
                    dve.wait_ge(r_ready, b)
                nc.vector.scalar_tensor_tensor(og[:], A[3][:], gamma_col, silu_g[:, b], ALU.mult,
                                               ALU.mult).then_inc(gated, 1)

            def add_x(b):
                dve.wait_ge(r_ready, b + 1)
                dve.wait_ge(o_rstd_ready, b + 1)
                if isinstance(b, int) and b == 0:
                    dve.wait_ge(beta_part_added, 1)
                for j in range(TILES):
                    nc.vector.scalar_tensor_tensor(A[0][:, tile(j)], A[0][:, tile(j)], o_rstd[:, j:j + 1],
                                                   x_tok[:, b, j], ALU.mult, ALU.add).then_inc(x1_ready, 1)
                dve.wait_ge(x1_ready, TILES * (b + 1))
                token_stats(b, A[0], r_stats, r_stats_ready)
                mean_and_variance(b, r_stats, r_stats_ready, r_mv, r_mv_ready, r_var, r_var_ready)

            def x2_normalise(b):
                dve.wait_ge(r_rstd_ready, b + 1)
                if not (isinstance(b, int) and b == 0):
                    dve.wait_ge(x2T_ready, b)
                    dve.wait_ge(x2_kept, b)
                normalise(x2, x2_ready, A[0], r_mv, r_rstd)

            def rest_of_x2(b):
                dve.wait_ge(x2_hi_ready, b + 1)
                nc.vector.tensor_tensor(x2_lo[:], A[1][:], x2_hi[:].bitcast(F32), ALU.subtract).then_inc(x2_lo_ready, 1)

            def ffn_product(b, o):
                bank = F[(2 * o + 1) % 4]
                dve.wait_ge(b_ready, OB * b + o + 1)
                dve.wait_ge(silu_a_ready, OB * b + o + 1)
                nc.vector.scalar_tensor_tensor(full_block(0, o), bank[:], scales[:, 1, o:o + 1], full[:, o % SLOTS],
                                               ALU.mult, ALU.mult).then_inc(f1_ready, 1)

            def rest(b, layer, o):
                if (layer, o) in ON_POOL:
                    return
                if layer == 0:
                    dve.wait_ge(f1_hi_ready, OB * b + o + 1)
                else:
                    dve.wait_ge(gelu_ready, 2 * OB * b + OB * (layer - 1) + o + 1)
                hi, lo = hidden[layer]
                nc.vector.tensor_tensor(lo[:, o], full_block(layer, o), hi[:, o].bitcast(F32),
                                        ALU.subtract).then_inc(dve_rested, 1)

            def add_x2(b):
                dve.wait_ge(y_tok_ready, b + 1)
                dve.wait_ge(x2_kept, b + 1)
                nc.vector.tensor_tensor(out_tok[:, b].rearrange("p j c -> p (j c)"), Y_BANK[:],
                                        x_tok[:, b].rearrange("p j c -> p (j c)"), ALU.add).then_inc(e_sum_ready, 1)

            def e_statistics(b):
                dve.wait_ge(e_sum_ready, b + 2)
                dve.sem_inc(stats_seen, 1)
                token_stats(b, out_tok[:, b].rearrange("p j c -> p (j c)"), e_stats, e_stats_ready)

            def e_mean_and_variance(b):
                mean_and_variance(b, e_stats, e_stats_ready, e_mv, e_mv_ready, e_var, e_var_ready)
                nc.vector.tensor_scalar(e_minus[:], e_mv[:, :, 0], -1.0, 1.0, ALU.mult,
                                        ALU.mult).then_inc(e_minus_ready, 1)

            def flag_lo():
                dve.wait_ge(lo_count_ready, 1)
                nc.vector.tensor_scalar(lo_flag[:], A[1][0:1, 0:1], 1.0, 0.0, ALU.min,
                                        ALU.max).then_inc(lo_flag_ready, 1)
                dve.wait_ge(lo_flag_ready, 1)

            def weight_bank_lo(n):
                dve.wait_ge(wT_hi_ready, n + 1)
                _, hi, lo, _ = weight_banks[n]
                nc.vector.tensor_tensor(lo, W_BANK[n][:], hi.bitcast(F32), ALU.subtract).then_inc(wT_lo_ready, 1)

            def first_layer(b, f, follows):
                ffn_product(b, 0)
                ffn_product(b, 1)
                if f is not None:
                    add_x2(f)
                ffn_product(b, 2)
                if follows:
                    scan(b + 1, 2)
                ffn_product(b, 3)
                if follows:
                    read_out(b + 1, 1)
                rest(b, 0, 3)
                if follows:
                    scan(b + 1, 3)
                if follows:
                    read_out(b + 1, 2)

            def attention_end(a, f, e):
                scan(a, 4)
                read_out(a, 3)
                scan(a, 5)
                read_out(a, 4)
                scan(a, 6)
                read_out(a, 5)
                if e is not None:
                    e_statistics(e)
                scan(a, 7)
                read_out(a, 6)
                read_out(a, 7)
                last_sums(a)
                if e is not None:
                    e_mean_and_variance(e)
                rest(f, 1, 2)

            def make_x2(a, f, follows):
                apply_gate(a)
                o_token_stats(a)
                rest(f, 1, 3)
                o_mean_and_variance(a)
                if follows:
                    outer_product(a + 1, LATER_U_ON_DVE)
                add_x(a)
                rest(f, 2, 0)
                rest(f, 2, 1)
                x2_normalise(a)
                rest(f, 2, 2)
                rest(f, 2, 3)
                rest_of_x2(a)

            dve.sem_inc(out_ready, 1)
            dve.sem_inc(e_sum_ready, 1)
            dve.sem_inc(yT_ready, 1)
            rest_of_x(0)
            dve.wait_ge(proj_hi_ready, 1)
            nc.vector.tensor_tensor(proj_lo[:, 0:2], proj_raw[:, 0:2], proj_hi[:, 0:2].bitcast(F32),
                                    ALU.subtract).then_inc(proj_lo_ready, 1)
            dve.wait_ge(proj_hi_ready, 2)
            nc.vector.tensor_tensor(proj_lo[:, 4], A[3][:, P:2 * P], proj_hi[:, 4].bitcast(F32),
                                    ALU.subtract).then_inc(proj_lo_ready, 1)
            dve.wait_ge(bias_hi_ready, 1)
            nc.vector.tensor_tensor(bias_lo[:], bias_row[:], bias_hi[:].bitcast(F32),
                                    ALU.subtract).then_inc(bias_lo_ready, 1)
            outer_product(0, U_ON_DVE[0])
            dve.wait_ge(proj_hi_ready, 3)
            nc.vector.tensor_tensor(proj_lo[:, 2:4], proj_raw[:, 2:4], proj_hi[:, 2:4].bitcast(F32),
                                    ALU.subtract).then_inc(proj_lo_ready, 1)
            outer_product(0, U_ON_DVE[1])
            log_gate(0)
            rest_of_q(0)
            rest_of_x(1)
            scan(0, 0)
            scan(0, 1)
            read_out(0, 0)
            rest_of_x(2)
            read_out(0, 1)
            scan(0, 2)
            rest_of_x(3)
            scan(0, 3)
            read_out(0, 2)
            log_gate(1)
            scan(0, 4)
            read_out(0, 3)
            scan(0, 5)
            read_out(0, 4)
            log_gate(2)
            scan(0, 6)
            read_out(0, 5)
            log_gate(3)
            scan(0, 7)
            read_out(0, 6)
            rest_of_q(1)
            read_out(0, 7)
            last_sums(0)
            weight_bank_lo(0)
            o_token_stats(0)
            o_mean_and_variance(0)
            apply_gate(0)
            weight_bank_lo(1)
            rest_of_q(2)
            add_beta_part(0)
            add_x(0)
            rest_of_q(3)
            weight_bank_lo(2)
            x2_normalise(0)
            weight_bank_lo(3)
            weight_bank_lo(4)
            add_beta_part(1)
            rest_of_x2(0)
            add_beta_part(2)
            add_beta_part(3)
            weight_bank_lo(5)
            weight_bank_lo(6)
            weight_bank_lo(7)
            scan(1, 0)
            weight_bank_lo(8)
            weight_bank_lo(9)
            scan(1, 1)
            weight_bank_lo(10)
            ffn_product(0, 0)
            read_out(1, 0)
            ffn_product(0, 1)
            scan(1, 2)
            ffn_product(0, 2)
            dve.wait_ge(lo_summed, len(lo_groups))
            nc.vector.tensor_scalar(lo_any[:], lo_sums[:], 0.0, 1.0, ALU.not_equal, ALU.mult).then_inc(lo_any_ready, 1)
            flag_lo()
            ffn_product(0, 3)
            read_out(1, 1)
            rest(0, 0, OB - 1)
            scan(1, 3)
            read_out(1, 2)

            attention_end(1, 0, None)
            with dve.Fori(0, B - 2) as i:
                make_x2(i + 1, i, True)
                scan(i + 2, 0)
                scan(i + 2, 1)
                read_out(i + 2, 0)
                first_layer(i + 1, i, True)
                attention_end(i + 2, i + 1, i)
            make_x2(B - 1, B - 2, False)
            first_layer(B - 1, B - 2, False)
            e_statistics(B - 2)
            e_mean_and_variance(B - 2)

            last_row = B - 1
            for layer in (1, 2):
                for o in range(OB):
                    rest(last_row, layer, o)
            for h in range(2):
                pair = slice(2 * h, 2 * h + 2)
                dve.wait_ge(y_tok_ready, B + h)
                dve.wait_ge(x2_kept, B)
                nc.vector.tensor_tensor(out_tok[:, last_row, pair].rearrange("p j c -> p (j c)"),
                                        LAST_Y[h][:, HALVES[h]], x_tok[:, last_row, pair].rearrange("p j c -> p (j c)"),
                                        ALU.add).then_inc(e_sum_ready, 1)
                dve.wait_ge(e_sum_ready, B + 1 + h)
                for j in (2 * h, 2 * h + 1):
                    nc.vector.bn_stats(e_stats[:, j], out_tok[:, last_row, j]).then_inc(e_stats_ready, 1)
                dve.wait_ge(e_stats_ready, TILES * last_row + 2 * (h + 1))
                for j in (2 * h, 2 * h + 1):
                    nc.vector.bn_aggr(e_mv[:, j], e_stats[:, j]).then_inc(e_mv_ready, 1)
                dve.wait_ge(e_mv_ready, TILES * last_row + 2 * (h + 1))
                nc.vector.tensor_tensor(e_var[:, pair], e_mv[:, pair, 1], eps[:, pair], ALU.add).then_inc(e_var_ready, 1)
                nc.vector.tensor_scalar(e_minus[:, pair], e_mv[:, pair, 0], -1.0, 1.0, ALU.mult,
                                        ALU.mult).then_inc(e_minus_ready, 1)


_INS = ['L0_attn_x', 'L0_attn_Wq', 'L0_attn_Wk', 'L0_attn_Wv', 'L0_attn_Wg', 'L0_attn_Wgk1', 'L0_attn_Wgk2',
        'L0_attn_bgk2', 'L0_attn_gamma', 'L0_attn_beta', 'L0_attn_Wout', 'L0_ffn_w1_w', 'L0_ffn_w1_s',
        'L0_ffn_w2_w', 'L0_ffn_w2_s', 'L0_ffn_h1_w', 'L0_ffn_h1_s', 'L0_ffn_h2_w', 'L0_ffn_h2_s',
        'L0_ffn_w3_w', 'L0_ffn_w3_s']


def kernel(**inputs):
    import numpy as np
    import concourse.bacc as bacc
    from concourse.bass_utils import run_bass_kernel_spmd

    nc = bacc.Bacc("TRN2", target_bir_lowering=False, num_devices=1)
    arrays, args = {}, []
    for name in _INS:
        a = np.ascontiguousarray(inputs[name])
        arrays[f"in_{name}"] = a
        args.append(nc.dram_tensor(f"in_{name}", a.shape, mybir.dt.from_np(a.dtype), kind="ExternalInput").ap())
    out = nc.dram_tensor("out_0", inputs['L0_attn_x'].shape, F32, kind="ExternalOutput").ap()
    gla_ffn_kernel(nc, *args, out)
    r = run_bass_kernel_spmd(nc, [arrays], core_ids=[0])
    return r.results[0]["out_0"]
```
